# Optimizing a Trainium2 kernel written in Bass

```python
import numpy as np
import jax
import jax.numpy as jnp

def _softmax(x, axis=-1):
    return jax.nn.softmax(x, axis=axis)
def _gelu(x):
    return jax.nn.gelu(x, approximate=True)
def _silu(x):
    return jax.nn.silu(x)
def _sigmoid(x):
    return jax.nn.sigmoid(x)
def _layernorm(x, axis=-1, eps=1e-5):
    m = jnp.mean(x, axis=axis, keepdims=True)
    v = jnp.var(x, axis=axis, keepdims=True)
    return (x - m) / jnp.sqrt(v + eps)
def _scatter_add(tgt, idx, src, axis=0):
    return tgt.at[idx].add(src)
def _segment_sum(src, seg, n):
    return jax.ops.segment_sum(src, seg, n)

kernel_name = 'mk_adj_preln_d2_adj_256_6cda51'

def setup_inputs(seed: int = 0):
    np.random.seed(seed)
    _w = jnp.asarray
    def _rec_inputs():
        import jax
        import jax.numpy as jnp
        _gk = jax.random.key(seed)
        x = -0.0005207 + 1.001 * jax.random.normal(jax.random.fold_in(_gk, 1), (8, 2048, 256), jnp.float32)
        _a = jax.random.bernoulli(jax.random.fold_in(_gk, 2), 0.0078125, (2048, 2048))
        adj = _a.astype(jnp.int32)
        return x, adj
    x, adj = _rec_inputs()
    def _L0_gnn_setup():
        import jax, jax.numpy as jnp
        import numpy as np
        import math
        CHUNK = 256
        NUM_HEADS = 4
        EPS = 1e-05
        key = jax.random.key(seed)
        ks = jax.random.split(key, 12)
        B, N, F = (4, 2048, 256)
        x = jax.random.normal(ks[0], (B, N, F), dtype=jnp.float32)
        adj_matrix = jax.random.randint(ks[1], (N, N), 0, 2, dtype=jnp.int32)
        s = 1.0 / math.sqrt(F)
        Wq = jax.random.normal(ks[2], (F, F), dtype=jnp.float32) * s
        bq = jnp.zeros((F,), dtype=jnp.float32)
        Wk = jax.random.normal(ks[3], (F, F), dtype=jnp.float32) * s
        bk = jnp.zeros((F,), dtype=jnp.float32)
        Wv = jax.random.normal(ks[4], (F, F), dtype=jnp.float32) * s
        bv = jnp.zeros((F,), dtype=jnp.float32)
        Wo = jax.random.normal(ks[5], (F, F), dtype=jnp.float32) * s
        bo = jnp.zeros((F,), dtype=jnp.float32)
        gamma = jnp.ones((F,), dtype=jnp.float32)
        beta = jnp.zeros((F,), dtype=jnp.float32)
        return {'x': x, 'adj_matrix': adj_matrix, 'Wq': Wq, 'bq': bq, 'Wk': Wk, 'bk': bk, 'Wv': Wv, 'bv': bv, 'Wo': Wo, 'bo': bo, 'gamma': gamma, 'beta': beta}
    _L0_gnn_all = _L0_gnn_setup()
    _L0_gnn_in = {k: v for k, v in _L0_gnn_all.items() if k in ('Wq', 'bq', 'Wk', 'bk', 'Wv', 'bv', 'Wo', 'bo', 'gamma', 'beta', )}
    del _L0_gnn_all

    def _L1_gnn_setup():
        import jax, jax.numpy as jnp
        import numpy as np
        B, N, F_IN, F_OUT = (8, 2048, 256, 256)
        key = jax.random.key(seed)
        k1, k2, k3, k4 = jax.random.split(key, 4)
        x = jax.random.normal(k1, (B, N, F_IN), dtype=jnp.float32)
        W = jax.random.normal(k2, (F_IN, F_OUT), dtype=jnp.float32) * (1.0 / np.sqrt(F_IN))
        a = jax.random.normal(k3, (2 * F_OUT, 1), dtype=jnp.float32) * (1.0 / np.sqrt(2 * F_OUT))
        adj = jax.random.randint(k4, (N, N), 0, 2, dtype=jnp.int32)
        return {'x': x, 'W': W, 'a': a, 'adj': adj}
    _L1_gnn_all = _L1_gnn_setup()
    _L1_gnn_in = {k: v for k, v in _L1_gnn_all.items() if k in ('W', 'a', )}
    del _L1_gnn_all

    return {
        "x": x,
        "adj": adj,
        "L0_gnn_Wq": _L0_gnn_in["Wq"],
        "L0_gnn_bq": _L0_gnn_in["bq"],
        "L0_gnn_Wk": _L0_gnn_in["Wk"],
        "L0_gnn_bk": _L0_gnn_in["bk"],
        "L0_gnn_Wv": _L0_gnn_in["Wv"],
        "L0_gnn_bv": _L0_gnn_in["bv"],
        "L0_gnn_Wo": _L0_gnn_in["Wo"],
        "L0_gnn_bo": _L0_gnn_in["bo"],
        "L0_gnn_gamma": _L0_gnn_in["gamma"],
        "L0_gnn_beta": _L0_gnn_in["beta"],
        "L1_gnn_W": _L1_gnn_in["W"],
        "L1_gnn_a": _L1_gnn_in["a"],
    }

def reference(x, adj, L0_gnn_Wq, L0_gnn_bq, L0_gnn_Wk, L0_gnn_bk, L0_gnn_Wv, L0_gnn_bv, L0_gnn_Wo, L0_gnn_bo, L0_gnn_gamma, L0_gnn_beta, L1_gnn_W, L1_gnn_a):
    import jax
    import jax.numpy as jnp
    def _L0_gnn_ref(x, adj_matrix, Wq, bq, Wk, bk, Wv, bv, Wo, bo, gamma, beta):
        import jax, jax.numpy as jnp
        import numpy as np
        import math
        CHUNK = 256
        NUM_HEADS = 4
        EPS = 1e-05
        B, N, Fin = x.shape
        H = NUM_HEADS
        Dout = Wq.shape[0]
        Dh = Dout // H
        Nc = N // CHUNK
        q = (x @ Wq.T + bq).reshape(B, N, H, Dh).transpose(0, 2, 1, 3)
        k = (x @ Wk.T + bk).reshape(B, N, H, Dh).transpose(0, 2, 1, 3)
        v = (x @ Wv.T + bv).reshape(B, N, H, Dh).transpose(0, 2, 1, 3)
        kc = k.reshape(B, H, Nc, CHUNK, Dh)
        vc = v.reshape(B, H, Nc, CHUNK, Dh)
        scores = jnp.einsum('bhnd,bhjcd->bhnjc', q, kc) / jnp.sqrt(jnp.asarray(Dh, dtype=q.dtype))
        scores = jnp.clip(scores, -10.0, 10.0)
        mask = adj_matrix.reshape(N, Nc, CHUNK)[None, None]
        scores = jnp.where(mask == 0, jnp.asarray(-10.0, scores.dtype), scores)
        attn = jax.nn.softmax(scores, axis=-1)
        ctx = jnp.einsum('bhnjc,bhjcd->bhnd', attn, vc)
        ctx = ctx.transpose(0, 2, 1, 3).reshape(B, N, Dout)
        out = ctx @ Wo.T + bo
        out = out + x
        mu = jnp.mean(out, axis=-1, keepdims=True)
        var = jnp.mean(jnp.square(out - mu), axis=-1, keepdims=True)
        out = (out - mu) * jax.lax.rsqrt(var + EPS) * gamma + beta
        return out

    def _L1_gnn_ref(x, W, a, adj):
        import jax, jax.numpy as jnp
        import numpy as np
        B, N, F_IN, F_OUT = (8, 2048, 256, 256)
        h = jnp.einsum('bnf,fo->bno', x, W)
        F = W.shape[1]
        a1 = a[:F, 0]
        a2 = a[F:, 0]
        s1 = jnp.einsum('bno,o->bn', h, a1)
        s2 = jnp.einsum('bno,o->bn', h, a2)
        e = jax.nn.leaky_relu(s1[:, :, None] + s2[:, None, :], negative_slope=0.2)
        mask = adj.astype(h.dtype)[None, :, :]
        e = e + (1.0 - mask) * -1000000000.0
        attention = jax.nn.softmax(e, axis=-1)
        out = jnp.einsum('bnm,bmo->bno', attention, h)
        return out

    h = jnp.maximum(_layernorm(x, axis=-1), 0.0)
    x = x + _L0_gnn_ref(h, adj, L0_gnn_Wq, L0_gnn_bq, L0_gnn_Wk, L0_gnn_bk, L0_gnn_Wv, L0_gnn_bv, L0_gnn_Wo, L0_gnn_bo, L0_gnn_gamma, L0_gnn_beta)
    h = jnp.maximum(_layernorm(x, axis=-1), 0.0)
    x = x + _L1_gnn_ref(h, L1_gnn_W, L1_gnn_a, adj)
    return x


_drawn_inputs = setup_inputs


def setup_inputs(seed=0):
    import zlib

    import numpy as np

    out = dict(_drawn_inputs(seed))
    spreads = {'L0_gnn_bq': (0.0, 0.8),
     'L0_gnn_bk': (0.0, 0.8),
     'L0_gnn_bv': (0.0, 0.1),
     'L0_gnn_bo': (0.0, 0.43),
     'L0_gnn_gamma': (1.0, 0.2),
     'L0_gnn_beta': (0.0, 0.1)}
    factors = {}
    for name, (base, spread) in spreads.items():
        noise = np.random.default_rng([zlib.crc32(name.encode()), seed]).standard_normal(out[name].shape)
        drawn = base * np.exp(spread * noise) if base else spread * noise
        out[name] = jnp.asarray(drawn.astype(out[name].dtype))
    for name, factor in factors.items():
        out[name] = (out[name] * factor).astype(out[name].dtype)
    return out
```

```python
from contextlib import ExitStack

import concourse.bass as bass
from concourse import mybir

F32 = mybir.dt.float32
F16 = mybir.dt.float16
BF16 = mybir.dt.bfloat16
U8 = mybir.dt.uint8
I32 = mybir.dt.int32
ALU = mybir.AluOpType
ACT = mybir.ActivationFunctionType
AX_X = mybir.AxisListType.X
RMAX = bass.bass_isa.ReduceOp.max

P = 128
EPS = 1e-5
CLIP = 10.0
EXP_HI = 22026.465794806718
EXP_LO = 4.5399929762484854e-05
SLOPE = 0.2
R_CAP = 100.0
CREDIT = 4


def gnn_two_layers(nc, x, adj_t, wq_t, bq, wk_t, bk, wv_t, bv, wo_t, bo, gamma, beta, w1, a1, out):
    B, N, F = x.shape
    G = 512
    T = G // P
    NG = N // G
    NB = N // P
    KB = F // P
    DH = 64
    HEADS = F // DH
    PAIRS = HEADS // 2
    CHUNK = 256
    CH = N // CHUNK
    CB = CHUNK // P
    SLOTS = CH * PAIRS
    UNITS = 2 * SLOTS
    W1C = F + 2
    HC = F + 1

    kq_d = nc.dram_tensor("kq_scratch", (B, 4, F, N), F16, kind="Internal").ap()
    hb_d = nc.dram_tensor("hb_scratch", (B, N, F), F32, kind="Internal").ap()
    xb_d = nc.dram_tensor("xb_scratch", (B, N, F), F32, kind="Internal").ap()
    x1_d = nc.dram_tensor("x1_scratch", (B, N, F), F32, kind="Internal").ap()
    s1_d = nc.dram_tensor("s1_scratch", (B, 1, N), F32, kind="Internal").ap()

    def rows(t, b, g):
        return t[b, bass.ds(g * G, G), :].rearrange("(t p) f -> p t f", p=P)

    with ExitStack() as ctx:
        def sb(name, shape, dt):
            return ctx.enter_context(nc.sbuf_tensor(name, shape, dt))

        def pb(name, shape):
            return ctx.enter_context(nc.psum_tensor(name, shape, F32))

        def sem(name):
            return ctx.enter_context(nc.semaphore(name))

        mask = sb("mask", [P, NB, N], U8)
        no_nb = sb("no_nb", [P, N], BF16)
        wqkv = [sb(f"w_{n}", [P, 2, KB, F], F16) for n in "qkv"]
        w1s = sb("w1s", [P, 2, KB, W1C], F16)
        wo = sb("wo", [P, KB, F], F32)
        bias_qk = sb("bias_qk", [P, 2, KB], F32)
        bv_b = sb("bv_b", [P, F], F32)
        bo_b = sb("bo_b", [P, F], F32)
        gamma_b = sb("gamma_b", [P, F], F32)
        beta_b = sb("beta_b", [P, F], F32)
        ident = sb("ident", [P, P], F32)
        ones = sb("ones", [P, DH], F32)
        ones_bf = sb("ones_bf", [P, P], BF16)
        minus_half = sb("minus_half", [P, T], F32)
        exp_lo = sb("exp_lo", [P, 1], F32)
        ks = sb("ks", [P, HEADS, N], F16)
        v = sb("v", [P, NB, F], F32)
        h2 = sb("h2", [P, NB, HC], F32)
        s2c = sb("s2c", [P, NB], F32)
        xg = [sb(f"xg{i}", [P, T, F], F32) for i in range(2)]
        hg = sb("hg", [P, T, F], F32)
        ht = sb("ht", [P, 2, KB * G], F16)
        kq_s = sb("kq_s", [P, 4, KB, G], F16)
        hb_s = sb("hb_s", [P, T, F], F32)
        xb_s = sb("xb_s", [P, T, F], F32)
        ln = sb("ln", [P, 16 * T], F32)
        limit = [sb(f"limit{i}", [P, CB, G], F32) for i in range(3)]
        qs = sb("qs", [P, 2, HEADS, G], F16)
        probs = sb("probs", [P, 4, CB * G], F32)
        presum = sb("presum", [P, 4, G], F32)
        den = sb("den", [P, G], F32)
        quot = sb("quot", [P, G], F32)
        acc = sb("acc", [P, PAIRS, G], F32)
        ctx_t = sb("ctx_t", [P, PAIRS, G], F32)
        tg = sb("tg", [P, T, F], F32)
        xbg = sb("xbg", [P, T, F], F32)
        x1g = sb("x1g", [P, T, F], F32)
        h1t = sb("h1t", [P, 2, KB, G], F16)
        s1row = sb("s1row", [1, G], F32)
        lt = sb("lt", [P, 16 * T], F32)
        mx = sb("mx", [P, 2], F32)
        s2m = sb("s2m", [P, NB], F32)
        b12 = sb("b12", [P, 2, NB], F32)
        hs = sb("hs", [P, HC], F32)
        hs_r = sb("hs_r", [P, HC], F32)
        hs3 = sb("hs3", [P, 3, HC], BF16)
        x1t = sb("x1t", [P, T, F], F32)
        og = sb("og", [P, T, F], F32)
        rden = sb("rden", [P, T], F32)
        rvec = probs[:, 2:4, :].rearrange("p a n -> p (a n)")
        prob1 = probs[:, 0:2, :].rearrange("p a (c n) -> p (a c) n", c=CB)
        scaled = presum

        ps_s = [pb(f"ps_s{i}", [P, CB * G]) for i in range(2)]
        ps_n = [pb(f"ps_n{i}", [P, G]) for i in range(2)]
        ps_d = pb("ps_d", [P, G])
        ps_x = pb("ps_x", [P, G])
        acc1 = [ps_s[t // 2][:, G * (t % 2):G * (t % 2) + HC] for t in range(T)]

        const_in = sem("const_in")
        wst_in = [sem(f"wst_in{i}") for i in range(2)]
        wst_used = sem("wst_used")
        adj_in = [sem(f"adj_in{i}") for i in range(2)]
        adj_used = sem("adj_used")
        pool_set = sem("pool_set")
        mask_bf_ready = sem("mask_bf_ready")
        count_done = sem("count_done")
        setup_done = sem("setup_done")
        step = sem("step")
        x_in = [sem(f"x_in{i}") for i in range(2)]
        var_a = sem("var_a")
        inv_a = sem("inv_a")
        stats_a = sem("stats_a")
        h_ready = sem("h_ready")
        hbxb_ready = sem("hbxb_ready")
        hbxb_out = sem("hbxb_out")
        h_turned = sem("h_turned")
        ht_hi = sem("ht_hi")
        ht_ready = sem("ht_ready")
        proj_ready = sem("proj_ready")
        kq_hi = sem("kq_hi")
        kq_ready = sem("kq_ready")
        kq_out = sem("kq_out")
        v_ready = sem("v_ready")
        ks_in = sem("ks_in")
        q_in = [sem(f"q_in{i}") for i in range(PAIRS)]
        limit_ready = sem("limit_ready")
        scores_ready = sem("scores_ready")
        exp_ready = sem("exp_ready")
        probs_ready = sem("probs_ready")
        presum_ready = sem("presum_ready")
        num_ready = sem("num_ready")
        den_sum = sem("den_sum")
        den_ready = sem("den_ready")
        divided = sem("divided")
        ctx_ready = sem("ctx_ready")
        tail_in = sem("tail_in")
        tail_mm = sem("tail_mm")
        tail_taken = sem("tail_taken")
        var_t = sem("var_t")
        inv_t = sem("inv_t")
        stats_t = sem("stats_t")
        y_ready = sem("y_ready")
        pool_step = sem("pool_step")
        x1_ready = sem("x1_ready")
        x1_out = sem("x1_out")
        var_u = sem("var_u")
        inv_u = sem("inv_u")
        stats_u = sem("stats_u")
        h1_ready = sem("h1_ready")
        h1t_hi = sem("h1t_hi")
        h1t_ready = sem("h1t_ready")
        s1_out = sem("s1_out")
        s2_max = sem("s2_max")
        s2_all = sem("s2_all")
        s2m_ready = sem("s2m_ready")
        b12_ready = sem("b12_ready")
        s1_in = sem("s1_in")
        s1_cap = sem("s1_cap")
        r_ready = sem("r_ready")
        hs_ready = sem("hs_ready")
        scaled_ready = sem("scaled_ready")
        prob1_ready = sem("prob1_ready")
        prob1_used = sem("prob1_used")
        agg_ready = sem("agg_ready")
        x1_in = sem("x1_in")
        out_ready = sem("out_ready")
        out_done = sem("out_done")

        block = ctx.enter_context(nc.Block())

        def hold(eng):
            eng.nop(nofuse=True)

        wst = [xg[0][:, 0:KB, :], xg[1][:, 0:KB, :]]
        a1_b = [hg[:, i, :] for i in range(2)]
        adj_st = [probs[:, 2 * i:2 * i + 2, :].rearrange("p a n -> p (a n)").bitcast(I32) for i in range(2)]
        mask_bf = [presum[:, 2 * i:2 * i + 2, :].rearrange("p a n -> p (a n)").bitcast(BF16) for i in range(2)]

        @block.sync
        def _(sp):
            def load_const(dst, src):
                sp.dma_start(dst, src).then_inc(const_in, 16)

            load_const(wo[:, :, :], wo_t.rearrange("(k p) o -> p k o", p=P))
            for i, t in enumerate((bq, bk)):
                with nc.allow_non_contiguous_dma(reason="one small column per partition"):
                    load_const(bias_qk[:, i, :], t.rearrange("(k p) -> p k", p=P))
            for dst, t in ((bv_b, bv), (bo_b, bo), (gamma_b, gamma), (beta_b, beta)):
                load_const(dst[:, :], t.rearrange("(a f) -> a f", a=1).to_broadcast([P, F]))
            for i in range(2):
                load_const(a1_b[i], a1[i:i + 1, :].to_broadcast([P, F]))
            for i, w in enumerate((wq_t, wk_t, wv_t, w1)):
                if i >= 2:
                    sp.wait_ge(wst_used, i - 1)
                sp.dma_start(wst[i % 2], w.rearrange("(k p) o -> p k o", p=P)).then_inc(wst_in[i % 2], 16)
            for c in range(NB):
                if c >= 2:
                    sp.wait_ge(adj_used, c - 1)
                sp.dma_start(adj_st[c % 2], adj_t[c * P:(c + 1) * P, :]).then_inc(adj_in[c % 2], 16)
            sp.wait_ge(setup_done, 1)

            def load_x(b, g, buf):
                sp.dma_start(xg[buf][:, :, :], rows(x, b, g)).then_inc(x_in[buf], 16)

            def store_projected(b, g, gi):
                sp.wait_ge(hbxb_ready, 2 * gi + 2)
                sp.dma_start(rows(hb_d, b, g), hb_s[:, :, :]).then_inc(hbxb_out, 16)
                sp.dma_start(rows(xb_d, b, g), xb_s[:, :, :]).then_inc(hbxb_out, 16)
                sp.wait_ge(kq_ready, 4 * gi + 4)
                for i in range(4):
                    sp.dma_start(kq_d[b, i, :, bass.ds(g * G, G)].rearrange("(k p) n -> p k n", p=P),
                                 kq_s[:, i, :, :]).then_inc(kq_out, 16)

            def load_q(b, g, pair):
                for half in range(2):
                    for part in range(2):
                        sp.dma_start(
                            qs[half * DH:(half + 1) * DH, part, 2 * pair:2 * pair + 2, :],
                            kq_d[b, 2 + part, 2 * pair * DH:(2 * pair + 2) * DH, bass.ds(g * G, G)]
                            .rearrange("(h d) n -> d h n", d=DH)).then_inc(q_in[pair], 16)

            def load_tail(b, g):
                sp.dma_start(tg[:, :, :], rows(hb_d, b, g)).then_inc(tail_in, 16)
                sp.dma_start(xbg[:, :, :], rows(xb_d, b, g)).then_inc(tail_in, 16)

            def store_tail(b, g, gi):
                sp.wait_ge(x1_ready, gi + 1)
                sp.dma_start(rows(x1_d, b, g), x1g[:, :, :]).then_inc(x1_out, 16)
                sp.wait_ge(tail_taken, 9 * gi + 9 + CREDIT)
                sp.dma_start(s1_d[b, :, bass.ds(g * G, G)], s1row[:, :]).then_inc(s1_out, 16)

            def store_out(b, g, gi):
                sp.wait_ge(out_ready, 4 * gi + 4 + CREDIT)
                sp.dma_start(rows(out, b, g), og[:, :, :]).then_inc(out_done, 16)

            with sp.Fori(0, B) as b:
                load_x(b, 0, 0)
                for g in range(NG):
                    gi = NG * b + g
                    if g + 1 < NG:
                        if g >= 1:
                            sp.wait_ge(hbxb_ready, 2 * gi)
                            sp.wait_ge(h_ready, gi)
                        load_x(b, g + 1, (g + 1) % 2)
                    store_projected(b, g, gi)
                sp.wait_ge(kq_out, 16 * 4 * (NG * b + NG))
                hold(sp)
                for part in range(2):
                    sp.dma_start(ks[part * DH:(part + 1) * DH, :, :],
                                 kq_d[b, part, :, :].rearrange("(h d) n -> d h n", d=DH)).then_inc(ks_in, 16)
                for pair in range(PAIRS):
                    load_q(b, 0, pair)
                sp.wait_ge(hbxb_out, 32 * (NG * b + NG))
                load_tail(b, 0)

                with sp.Fori(1, NG) as g:
                    gi = NG * b + g
                    for pair in range(PAIRS):
                        sp.wait_ge(scores_ready, UNITS * gi - 2 * (PAIRS - 1 - pair))
                        load_q(b, g, pair)
                    store_tail(b, g - 1, gi - 1)
                    load_tail(b, g)
                store_tail(b, NG - 1, NG * b + NG - 1)

                sp.wait_ge(s1_out, 16 * (NG * b + NG))
                sp.wait_ge(x1_out, 16 * (NG * b + NG))
                hold(sp)
                sp.dma_start(rvec, s1_d[b, :, :].to_broadcast([P, N])).then_inc(s1_in, 16)
                with sp.Fori(0, NG) as g:
                    gi = NG * b + g
                    sp.wait_ge(out_ready, 4 * gi + CREDIT)
                    sp.dma_start(x1t[:, :, :], rows(x1_d, b, g)).then_inc(x1_in, 16)
                    store_out(b, g, gi)
            sp.wait_ge(out_done, 16 * NG * B)

        def work_views(work):
            return (work[:, 0:6 * T].rearrange("p (t s) -> p t s", t=T), work[:, 6 * T:8 * T].rearrange("p (t s) -> p t s", t=T),
                    work[:, 8 * T:9 * T], work[:, 9 * T:10 * T], work[:, 10 * T:11 * T])

        def variances(dve, src, work, done, chain, n):
            st, mv, var, _, _ = work_views(work)
            for t in range(T):
                last = nc.vector.bn_stats(st[:, t, :], src[:, t, :])
            last.then_inc(chain, 1)
            dve.wait_ge(chain, n + 1)
            hold(dve)
            for t in range(T):
                last = nc.vector.bn_aggr(mv[:, t, :], st[:, t:t + 1, :])
            last.then_inc(chain, 1)
            dve.wait_ge(chain, n + 2)
            nc.vector.tensor_scalar(var, mv[:, :, 1], EPS, None, ALU.add).then_inc(done, 1)

        def inverse_deviations(work, done):
            _, _, var, inv, _ = work_views(work)
            nc.gpsimd.tensor_tensor(inv, var, minus_half[:, :], ALU.pow).then_inc(done, 1)

        def shifts(work, done):
            _, mv, _, inv, shift = work_views(work)
            nc.vector.scalar_tensor_tensor(out=shift, in0=mv[:, :, 0], scalar=-1.0, in1=inv,
                                           op0=ALU.mult, op1=ALU.mult).then_inc(done, 1)

        def norm_args(work, t):
            _, _, _, inv, shift = work_views(work)
            return dict(scale=inv[:, t:t + 1], bias=shift[:, t:t + 1])

        @block.gpsimd
        def _(pool):
            nc.gpsimd.memset(ident[:, :], 0.0).then_inc(pool_set, 1)
            pool.wait_ge(pool_set, 1)
            nc.gpsimd.affine_select(out=ident[:, :], in_=ident[:, :], compare_op=ALU.not_equal, fill=1.0,
                                    base=0, pattern=[[-1, P]], channel_multiplier=1).then_inc(pool_set, 1)
            nc.gpsimd.memset(minus_half[:, :], -0.5)
            nc.gpsimd.memset(h2[:, :, F:HC], 1.0).then_inc(pool_set, 1)
            pool.wait_ge(const_in, 16 * 9)
            pool.wait_ge(setup_done, 1)

            def save_residuals(gi, buf, xi):
                pool.wait_ge(var_a, gi + 1)
                pool.wait_ge(pool_set, 3)
                inverse_deviations(ln, inv_a)
                pool.wait_ge(hbxb_out, 32 * gi)
                pool.wait_ge(x_in[buf], 16 * xi)
                for t in range(T):
                    last = nc.gpsimd.tensor_tensor(xb_s[:, t, :], xg[buf][:, t, :], beta_b[:, :], ALU.add)
                last.then_inc(hbxb_ready, 1)
                pool.wait_ge(h_ready, gi + 1)
                for t in range(T):
                    last = nc.gpsimd.tensor_tensor(hb_s[:, t, :], hg[:, t, :], bo_b[:, :], ALU.add)
                last.then_inc(hbxb_ready, 1)

            def tail_x1(gi):
                pool.wait_ge(y_ready, gi + 1)
                pool.wait_ge(x1_out, 16 * gi)
                for t in range(T):
                    last = nc.gpsimd.tensor_tensor(x1g[:, t, :], tg[:, t, :], gamma_b[:, :], ALU.mult)
                last.then_inc(pool_step, 1)
                pool.wait_ge(pool_step, gi + 1)
                last = nc.gpsimd.tensor_tensor(x1g[:, :, :], x1g[:, :, :], xbg[:, :, :], ALU.add)
                last.then_inc(x1_ready, 1)

            def tail_step(gi, s):
                if s == 3:
                    pool.wait_ge(var_t, gi + 1)
                    inverse_deviations(lt, inv_t)
                if s == 5:
                    tail_x1(gi)
                if s == 7:
                    pool.wait_ge(var_u, gi + 1)
                    inverse_deviations(lt, inv_u)

            def attend(gi, g, tail):
                for s in range(SLOTS):
                    for u in (2 * s, 2 * s + 1):
                        pool.wait_ge(probs_ready, UNITS * gi + u + 1 + CREDIT)
                        pool.wait_ge(den_sum, SLOTS * gi + max(s - 1, 0))
                        nc.gpsimd.tensor_tensor(presum[:, u % 4, :], probs[:, u % 4, 0:G],
                                                probs[:, u % 4, G:2 * G], ALU.add).then_inc(presum_ready, 1)
                    if tail:
                        tail_step(gi - 1, s)

            with pool.Fori(0, B) as b:
                for g in range(NG):
                    save_residuals(NG * b + g, g % 2, NG // 2 * b + g // 2 + 1)
                attend(NG * b, 0, False)
                with pool.Fori(1, NG) as g:
                    attend(NG * b + g, g, True)
                for s in range(SLOTS):
                    tail_step(NG * b + NG - 1, s)
                pool.wait_ge(s2_max, b + 1)
                hold(pool)
                nc.gpsimd.partition_all_reduce(mx[:, 1:2], mx[:, 0:1], P, RMAX).then_inc(s2_all, 1)

        chain_a = sem("chain_a")
        chain_t = sem("chain_t")
        chain_u = sem("chain_u")
        chain_c = sem("chain_c")
        chain_d = sem("chain_d")

        @block.vector
        def _(dve):
            steps = [0]

            def link(ins):
                steps[0] += 1
                ins.then_inc(step, 1)
                dve.wait_ge(step, steps[0])

            for s, n in ((tail_taken, CREDIT), (probs_ready, CREDIT), (divided, CREDIT), (out_ready, CREDIT)):
                dve.sem_inc(s, n)
            nc.vector.memset(ones[:, :], 1.0)
            nc.vector.memset(exp_lo[:, :], EXP_LO)
            link(nc.vector.memset(ones_bf[:, :], 1.0))
            dve.wait_ge(const_in, 16 * 9)
            for i in range(4):
                dve.wait_ge(wst_in[i % 2], 16 * (i // 2 + 1))
                if i < 3:
                    dst, src = wqkv[i], wst[i % 2]
                else:
                    ext = tg[:, 0:3, :].rearrange("p t f -> p (t f)")[:, 0:KB * W1C].rearrange("p (k c) -> p k c", k=KB)
                    prod = x1g[:, 0:2 * KB, :]
                    for k in range(KB):
                        nc.vector.tensor_copy(ext[:, k, 0:F], wst[1][:, k, :])
                        for j in range(2):
                            last = nc.vector.tensor_tensor(prod[:, 2 * k + j, :], wst[1][:, k, :], a1_b[j], ALU.mult)
                    link(last)
                    for k in range(KB):
                        last = nc.vector.tensor_reduce(ext[:, k, F:F + 2], prod[:, 2 * k:2 * k + 2, :], AX_X, ALU.add)
                    link(last)
                    dst, src = w1s, ext
                link(nc.vector.tensor_copy(dst[:, 0, :, :], src))
                steps[0] += 1
                nc.vector.tensor_tensor(dst[:, 1, :, :], src, dst[:, 0, :, :], ALU.subtract).then_inc(step, 1)
                dve.wait_ge(step, steps[0])
                dve.sem_inc(wst_used, 1)
            for c in range(NB):
                dve.wait_ge(adj_in[c % 2], 16 * (c // 2 + 1))
                nc.vector.tensor_scalar(mask[:, c, :], adj_st[c % 2], 0, None, ALU.not_equal).then_inc(adj_used, 1)
                dve.wait_ge(adj_used, c + 1)
                if c >= 2:
                    dve.wait_ge(count_done, c - 1)
                nc.vector.tensor_copy(mask_bf[c % 2], mask[:, c, :]).then_inc(mask_bf_ready, 1)
            dve.wait_ge(count_done, NB)
            for i in range(2):
                last = nc.vector.tensor_scalar(no_nb[:, i * CB * G:(i + 1) * CB * G], ps_s[i][:, :], 0.5, None, ALU.is_lt)
                if i == 1:
                    last.then_inc(setup_done, 1)
                else:
                    link(last)

            def project(b, g, gi, buf, xi):
                dve.wait_ge(x_in[buf], 16 * xi)
                dve.wait_ge(h_ready, gi)
                variances(dve, xg[buf], ln, var_a, chain_a, 2 * gi)
                dve.wait_ge(inv_a, gi + 1)
                shifts(ln, stats_a)
                dve.wait_ge(ht_hi, gi + 1)
                nc.vector.tensor_tensor(ht[:, 1, :], ps_s[0][:, :], ht[:, 0, :], ALU.subtract).then_inc(ht_ready, 1)
                dve.wait_ge(kq_out, 64 * gi)
                for i, ps in enumerate((ps_n[0][:, :], ps_n[1][:, :], ps_s[1][:, 0:G], ps_s[1][:, G:2 * G])):
                    dve.wait_ge(kq_hi, 4 * gi + i + 1)
                    w, k = 1 - i // 2, i % 2
                    nc.vector.scalar_tensor_tensor(
                        out=kq_s[:, 2 * (i // 2) + 1, k, :], in0=ps, scalar=bias_qk[:, w, k:k + 1],
                        in1=kq_s[:, 2 * (i // 2), k, :], op0=ALU.add, op1=ALU.subtract).then_inc(kq_ready, 1)
                for i, ps in enumerate((ps_d, ps_x)):
                    dve.wait_ge(proj_ready, 6 * gi + 5 + i)
                    for t in range(2):
                        last = nc.vector.tensor_tensor(v[:, bass.ds(T * g + 2 * i + t, 1), :],
                                                       ps[:, t * F:(t + 1) * F].unsqueeze(1),
                                                       bv_b[:, :].unsqueeze(1), ALU.add)
                    last.then_inc(v_ready, 1)

            def bound(gi, u):
                dve.wait_ge(exp_ready, UNITS * gi + u + 1)
                if u % HEADS == 0:
                    dve.wait_ge(limit_ready, CH * gi + u // HEADS + 1)
                dve.wait_ge(presum_ready, UNITS * gi + max(u - 3, 0))
                dve.wait_ge(num_ready, SLOTS * gi + max(u // 2 - 1, 0))
                nc.vector.scalar_tensor_tensor(
                    out=probs[:, u % 4, :], in0=ps_s[u % 2][:, :], scalar=EXP_LO,
                    in1=limit[u // HEADS % 3][:, :, :].rearrange("p c n -> p (c n)"),
                    op0=ALU.max, op1=ALU.min).then_inc(probs_ready, 1)

            def divide(gi, s):
                c, p = s // PAIRS, s % PAIRS
                dve.wait_ge(divided, SLOTS * gi + s + CREDIT)
                dve.wait_ge(den_sum, SLOTS * gi + s + 1)
                nc.vector.reciprocal(den[:, :], ps_d[:, :]).then_inc(den_ready, 1)
                dve.wait_ge(den_ready, SLOTS * gi + s + 1)
                dve.wait_ge(num_ready, SLOTS * gi + s + 1)
                first = c == 0
                dve.wait_ge(chain_c, (SLOTS - PAIRS) * gi + max(s - PAIRS, 0))
                dst = acc[:, p, :] if first else quot[:, :]
                nc.vector.tensor_tensor(dst, ps_n[s % 2][:, :], den[:, :], ALU.mult).then_inc(divided, 1)
                if not first:
                    dve.wait_ge(divided, SLOTS * gi + s + 1 + CREDIT)
                    dst = ctx_t if c == CH - 1 else acc
                    nc.vector.tensor_tensor(dst[:, p, :], acc[:, p, :], quot[:, :], ALU.add).then_inc(chain_c, 1)

            def tail_add(gi, a):
                if a == 0:
                    dve.wait_ge(tail_in, 32 * gi + 32)
                dve.wait_ge(tail_mm, 9 * gi + a + 1)
                nc.vector.tensor_tensor(tg[:, 2 * a:2 * a + 2, :],
                                        ps_x[:, :].rearrange("p (t f) -> p t f", t=2),
                                        tg[:, 2 * a:2 * a + 2, :], ALU.add).then_inc(tail_taken, 1)

            def tail_stats(gi):
                dve.wait_ge(tail_taken, 9 * gi + 2 + CREDIT)
                variances(dve, tg, lt, var_t, chain_t, 2 * gi)

            def tail_stats1(gi):
                dve.wait_ge(x1_ready, gi + 1)
                variances(dve, x1g, lt, var_u, chain_u, 2 * gi)

            def tail_low(gi, k):
                dve.wait_ge(h1t_hi, KB * gi + k + 1)
                nc.vector.tensor_tensor(h1t[:, 1, k, :], ps_x[:, :], h1t[:, 0, k, :], ALU.subtract)\
                    .then_inc(tail_taken, 1)

            def attend(gi, tail):
                for u in range(2):
                    bound(gi, u)
                for s in range(SLOTS):
                    if s + 1 < SLOTS:
                        bound(gi, 2 * s + 2)
                        bound(gi, 2 * s + 3)
                    if s >= 1:
                        divide(gi, s - 1)
                    if tail:
                        tail_step(gi - 1, s)
                divide(gi, SLOTS - 1)

            def tail_step(gi, s):
                if s == 2:
                    tail_add(gi, 0)
                if s == 3:
                    tail_add(gi, 1)
                    tail_stats(gi)
                if s == 4:
                    dve.wait_ge(inv_t, gi + 1)
                    shifts(lt, stats_t)
                if s == 7:
                    tail_stats1(gi)
                if s == 8:
                    dve.wait_ge(inv_u, gi + 1)
                    shifts(lt, stats_u)
                if s in (11, 12):
                    tail_low(gi, s - 11)

            def aggregate(gi, mb):
                dve.wait_ge(scaled_ready, NB * gi + mb + 1)
                if mb == 3:
                    dve.wait_ge(agg_ready, T * gi)
                else:
                    dve.wait_ge(prob1_used, (NB - 1) * gi + (mb - 2 if mb < 3 else mb - 3) + CREDIT)
                nc.vector.scalar_tensor_tensor(
                    out=prob1[:, mb % 4, :], in0=scaled[:, mb % 4, :], scalar=b12[:, 1, mb:mb + 1],
                    in1=mask[:, mb, bass.ds(self_g[0] * G, G)], op0=ALU.max, op1=ALU.mult).then_inc(prob1_ready, 1)

            self_g = [0]

            def emit(gi):
                dve.wait_ge(x1_in, 16 * (gi + 1))
                dve.wait_ge(out_done, 16 * gi)
                for t in range(T):
                    dve.wait_ge(agg_ready, T * gi + t + 1)
                    dve.wait_ge(out_ready, T * gi + t + CREDIT)
                    nc.vector.reciprocal(rden[:, t:t + 1], acc1[t][:, F:HC]).then_inc(chain_d, 1)
                    dve.wait_ge(chain_d, T * gi + t + 1)
                    nc.vector.scalar_tensor_tensor(out=og[:, t, :], in0=acc1[t][:, 0:F], scalar=rden[:, t:t + 1],
                                                   in1=x1t[:, t, :], op0=ALU.mult, op1=ALU.add).then_inc(out_ready, 1)

            chain_s = sem("chain_s")
            S_LINKS = 6
            with dve.Fori(0, B) as b:
                for g in range(NG):
                    project(b, g, NG * b + g, g % 2, NG // 2 * b + g // 2 + 1)
                attend(NG * b, False)
                with dve.Fori(1, NG) as g:
                    attend(NG * b + g, True)
                gl = NG * b + NG - 1
                for s in range(SLOTS):
                    tail_step(gl, s)

                dve.wait_ge(tail_taken, 9 * gl + 9 + CREDIT)
                nc.vector.tensor_reduce(mx[:, 0:1], s2c[:, :], AX_X, ALU.max).then_inc(s2_max, 1)
                n = [0]

                def link_b(ins):
                    n[0] += 1
                    ins.then_inc(chain_s, 1)
                    dve.wait_ge(chain_s, S_LINKS * b + n[0])

                link_b(nc.vector.tensor_reduce(hs[:, :], h2[:, :, :].rearrange("p m f -> p f m"), AX_X, ALU.add))
                link_b(nc.vector.tensor_copy(hs3[:, 0, :], hs[:, :]))
                link_b(nc.vector.tensor_tensor(hs_r[:, :], hs[:, :], hs3[:, 0, :], ALU.subtract))
                link_b(nc.vector.tensor_copy(hs3[:, 1, :], hs_r[:, :]))
                link_b(nc.vector.tensor_tensor(hs[:, :], hs_r[:, :], hs3[:, 1, :], ALU.subtract))
                nc.vector.tensor_copy(hs3[:, 2, :], hs[:, :]).then_inc(hs_ready, 1)
                dve.wait_ge(s2_all, b + 1)
                nc.vector.tensor_scalar(s2m[:, :], s2c[:, :], mx[:, 1:2], None, ALU.subtract).then_inc(s2m_ready, 1)
                dve.wait_ge(s1_in, 16 * (b + 1))
                nc.vector.tensor_scalar(rvec, rvec, mx[:, 1:2], R_CAP, ALU.add, ALU.min).then_inc(s1_cap, 1)
                dve.wait_ge(b12_ready, 2 * b + 2)
                link_b(nc.vector.memset(rden[:, :], 0.0))

                self_g[0] = 0
                for mb in range(NB):
                    aggregate(NG * b, mb)
                with dve.Fori(1, NG) as g:
                    self_g[0] = g
                    for mb in range(NB):
                        aggregate(NG * b + g, mb)
                        if mb == 2:
                            emit(NG * b + g - 1)
                emit(gl)

        @block.scalar
        def _(act):
            def project(gi, buf):
                act.wait_ge(stats_a, gi + 1)
                act.wait_ge(h_turned, gi)
                act.wait_ge(hbxb_ready, 2 * gi)
                for t in range(T):
                    last = nc.scalar.activation(hg[:, t, :], xg[buf][:, t, :], ACT.Relu,
                                                **norm_args(ln, t))
                last.then_inc(h_ready, 1)
                act.wait_ge(h_turned, gi + 1)
                act.wait_ge(proj_ready, 6 * gi)
                nc.scalar.copy(ht[:, 0, :], ps_s[0][:, :]).then_inc(ht_hi, 1)
                act.wait_ge(kq_out, 64 * gi)
                for i, ps in enumerate((ps_n[0][:, :], ps_n[1][:, :], ps_s[1][:, 0:G], ps_s[1][:, G:2 * G])):
                    act.wait_ge(proj_ready, 6 * gi + i + 1)
                    w, k = 1 - i // 2, i % 2
                    nc.scalar.activation(kq_s[:, 2 * (i // 2), k, :], ps, ACT.Identity,
                                         bias=bias_qk[:, w, k:k + 1]).then_inc(kq_hi, 1)

            def exp(gi, u):
                act.wait_ge(scores_ready, UNITS * gi + u + 1)
                nc.scalar.activation(ps_s[u % 2][:, :], ps_s[u % 2][:, :], ACT.Exp, scale=DH ** -0.5).then_inc(exp_ready, 1)

            def normalise(gi):
                act.wait_ge(stats_t, gi + 1)
                for t in range(T):
                    last = nc.scalar.activation(tg[:, t, :], tg[:, t, :], ACT.Identity,
                                                **norm_args(lt, t))
                last.then_inc(y_ready, 1)

            def rectify(gi):
                act.wait_ge(stats_u, gi + 1)
                for t in range(T):
                    last = nc.scalar.activation(tg[:, t, :], x1g[:, t, :], ACT.Relu,
                                                **norm_args(lt, t))
                last.then_inc(h1_ready, 1)

            def tail_high(gi, k):
                act.wait_ge(tail_mm, 9 * gi + 3 + k)
                nc.scalar.copy(h1t[:, 0, k, :], ps_x[:, :]).then_inc(h1t_hi, 1)

            def take_features(gi, g, t):
                act.wait_ge(tail_mm, 9 * gi + 5 + t)
                hold(act)
                nc.scalar.copy(h2[:, bass.ds(T * g + t, 1), 0:F], ps_x[:, 0:F].unsqueeze(1))
                nc.scalar.copy(s2c[:, bass.ds(T * g + t, 1)], ps_x[:, F + 1:F + 2]).then_inc(tail_taken, 1)

            def take_s1(gi):
                act.wait_ge(tail_mm, 9 * gi + 9)
                act.wait_ge(s1_out, 16 * gi)
                nc.scalar.copy(s1row[:, :], ps_x[0:1, :]).then_inc(tail_taken, 1)

            def tail_step(gi, g, s):
                if s == 5:
                    normalise(gi)
                if s == 9:
                    rectify(gi)
                if s in (10, 11):
                    tail_high(gi, s - 10)
                if s in (12, 13, 14):
                    take_features(gi, g, s - 12)
                if s == 15:
                    take_features(gi, g, 3)
                    take_s1(gi)

            def expand(gi, g, c):
                act.wait_ge(probs_ready, UNITS * gi + (HEADS * (c - 2) if c >= 3 else 0) + CREDIT)
                hold(act)
                nc.scalar.activation(limit[c % 3][:, :, :], mask[:, CB * c:CB * c + CB, bass.ds(g * G, G)],
                                     ACT.Identity, scale=EXP_HI - EXP_LO, bias=exp_lo[:, :]).then_inc(limit_ready, 1)

            def attend(gi, g, tail):
                for c in range(2):
                    expand(gi, g, c)
                for u in range(2):
                    exp(gi, u)
                for s in range(SLOTS):
                    if s + 1 < SLOTS:
                        exp(gi, 2 * s + 2)
                        exp(gi, 2 * s + 3)
                    if s % 2 == 0 and s // 2 + 2 < CH:
                        expand(gi, g, s // 2 + 2)
                    if tail:
                        tail_step(gi - 1, g - 1, s)

            def scale(gi, g, mb):
                act.wait_ge(prob1_ready, NB * gi + mb - 3 if mb >= 4 else NB * gi)
                hold(act)
                nc.scalar.activation(scaled[:, mb % 4, :], rvec[:, bass.ds(g * G, G)], ACT.Copy,
                                     scale=b12[:, 0, mb:mb + 1]).then_inc(scaled_ready, 1)

            act.wait_ge(setup_done, 1)
            with act.Fori(0, B) as b:
                for g in range(NG):
                    project(NG * b + g, g % 2)
                attend(NG * b, 0, False)
                with act.Fori(1, NG) as g:
                    attend(NG * b + g, g, True)
                for s in range(SLOTS):
                    tail_step(NG * b + NG - 1, NG - 1, s)
                act.wait_ge(s2m_ready, b + 1)
                nc.scalar.activation(b12[:, 0, :], s2m[:, :], ACT.Exp).then_inc(b12_ready, 1)
                nc.scalar.activation(b12[:, 1, :], s2m[:, :], ACT.Exp, scale=SLOPE).then_inc(b12_ready, 1)
                act.wait_ge(s1_cap, b + 1)
                nc.scalar.activation(rvec, rvec, ACT.Exp, scale=1.0 - SLOPE).then_inc(r_ready, 1)
                act.wait_ge(b12_ready, 2 * b + 2)
                act.wait_ge(r_ready, b + 1)
                with act.Fori(0, NG) as g:
                    for mb in range(NB):
                        scale(NG * b + g, g, mb)

        @block.tensor
        def _(pe):
            PARTS = ((0, 0), (0, 1), (1, 0))

            pe.sem_inc(prob1_used, CREDIT)
            pe.wait_ge(step, 1)
            for c in range(NB):
                pe.wait_ge(mask_bf_ready, c + 1)
                for g in range(NG):
                    mm = nc.tensor.matmul(ps_s[g // 2][:, G * (g % 2):G * (g % 2) + G], ones_bf[:, :],
                                          mask_bf[c % 2][:, 0:N][:, g * G:(g + 1) * G],
                                          start=(c == 0), stop=(c == NB - 1))
                mm.then_inc(count_done, 1)
            pe.wait_ge(pool_set, 3)
            pe.wait_ge(setup_done, 1)

            def project(gi, t0):
                pe.wait_ge(h_ready, gi + 1)
                for k in range(KB):
                    for t in range(T):
                        mm = nc.tensor.transpose(ps_s[0][:, k * G + t * P:k * G + (t + 1) * P],
                                                 hg[:, t, k * P:(k + 1) * P], ident[:, :])
                mm.then_inc(h_turned, 1)
                pe.wait_ge(ht_ready, gi + 1)
                pe.wait_ge(kq_ready, 4 * gi)
                for i, ps in enumerate((ps_n[0][:, :], ps_n[1][:, :], ps_s[1][:, 0:G], ps_s[1][:, G:2 * G])):
                    w, fb = wqkv[1 - i // 2], i % 2
                    n = 0
                    for k in range(KB):
                        for a, c in PARTS:
                            mm = nc.tensor.matmul(ps, w[:, a, k, fb * P:(fb + 1) * P], ht[:, c, k * G:(k + 1) * G],
                                                  start=(n == 0), stop=(n == 3 * KB - 1))
                            n += 1
                    mm.then_inc(proj_ready, 1)
                pe.wait_ge(v_ready, 2 * gi)
                for i, ps in enumerate((ps_d, ps_x)):
                    for t in range(2):
                        n = 0
                        for k in range(KB):
                            for a, c in PARTS:
                                at = k * G + (2 * i + t) * P
                                mm = nc.tensor.matmul(ps[:, t * F:(t + 1) * F], ht[:, a, at:at + P], wqkv[2][:, c, k, :],
                                                      start=(n == 0), stop=(n == 3 * KB - 1))
                                n += 1
                    mm.then_inc(proj_ready, 1)

            def score(gi, b, u):
                h, c = u % HEADS, u // HEADS
                if c == 0 and h % 2 == 0:
                    pe.wait_ge(q_in[h // 2], 64 * (gi + 1))
                pe.wait_ge(probs_ready, UNITS * gi + u - 1 + (CREDIT - 0))
                for cb in range(CB):
                    for part in range(2):
                        mm = nc.tensor.matmul(ps_s[u % 2][:, cb * G:(cb + 1) * G],
                                              ks[:, h, (CB * c + cb) * P:(CB * c + cb + 1) * P],
                                              qs[:, part, h, :], start=(part == 0), stop=(part == 1))
                mm.then_inc(scores_ready, 1)

            def context(gi, s):
                c, p = s // PAIRS, s % PAIRS
                pe.wait_ge(probs_ready, UNITS * gi + 2 * s + 2 + CREDIT)
                pe.wait_ge(divided, SLOTS * gi + s - 1 + CREDIT)
                for cb in range(CB):
                    for h in range(2):
                        mm = nc.tensor.matmul(ps_n[s % 2][h * DH:(h + 1) * DH, :],
                                              v[:, CB * c + cb, (2 * p + h) * DH:(2 * p + h + 1) * DH],
                                              probs[:, (2 * s + h) % 4, cb * G:(cb + 1) * G],
                                              start=(cb == 0), stop=(cb == CB - 1))
                mm.then_inc(num_ready, 1)

            def denominator(gi, s):
                pe.wait_ge(presum_ready, UNITS * gi + 2 * s + 2)
                pe.wait_ge(den_ready, SLOTS * gi + s)
                for h in range(2):
                    mm = nc.tensor.matmul(ps_d[h * DH:(h + 1) * DH, :], ones[:, :], presum[:, (2 * s + h) % 4, :],
                                          start=True, stop=True)
                mm.then_inc(den_sum, 1)

            def tail_out(gi, a):
                if a == 0:
                    pe.wait_ge(chain_c, (SLOTS - PAIRS) * (gi + 1))
                pe.wait_ge(tail_taken, 9 * gi + a + CREDIT)
                for t in range(2):
                    for k in range(KB):
                        at = (2 * a + t) * P
                        mm = nc.tensor.matmul(ps_x[:, t * F:(t + 1) * F], ctx_t[:, k, at:at + P], wo[:, k, :],
                                              start=(k == 0), stop=(k == KB - 1))
                mm.then_inc(tail_mm, 1)

            def tail_turn(gi, k):
                if k == 0:
                    pe.wait_ge(h1_ready, gi + 1)
                pe.wait_ge(tail_taken, 9 * gi + 2 + k + CREDIT)
                for t in range(T):
                    mm = nc.tensor.transpose(ps_x[:, t * P:(t + 1) * P], tg[:, t, k * P:(k + 1) * P], ident[:, :])
                mm.then_inc(tail_mm, 1)

            def tail_features(gi, t):
                pe.wait_ge(tail_taken, 9 * gi + 4 + t + CREDIT)
                n = 0
                for k in range(KB):
                    for a, c in PARTS:
                        mm = nc.tensor.matmul(ps_x[:, 0:W1C], h1t[:, a, k, t * P:(t + 1) * P], w1s[:, c, k, :],
                                              start=(n == 0), stop=(n == 3 * KB - 1))
                        n += 1
                mm.then_inc(tail_mm, 1)

            def tail_s1(gi):
                pe.wait_ge(tail_taken, 9 * gi + 8 + CREDIT)
                n = 0
                for k in range(KB):
                    for a, c in PARTS:
                        mm = nc.tensor.matmul(ps_x[0:1, :], w1s[:, a, k, F:F + 1], h1t[:, c, k, :],
                                              start=(n == 0), stop=(n == 3 * KB - 1))
                        n += 1
                mm.then_inc(tail_mm, 1)

            def tail_step(gi, s):
                if s in (1, 2):
                    tail_out(gi, s - 1)
                if s in (10, 11):
                    tail_turn(gi, s - 10)
                if s in (12, 13, 14):
                    tail_features(gi, s - 12)
                if s == 15:
                    tail_features(gi, 3)
                    tail_s1(gi)

            def attend(gi, b, tail):
                for u in range(2):
                    score(gi, b, u)
                for s in range(SLOTS):
                    if s + 1 < SLOTS:
                        score(gi, b, 2 * s + 2)
                        score(gi, b, 2 * s + 3)
                    context(gi, s)
                    denominator(gi, s)
                    if tail:
                        tail_step(gi - 1, s)

            def aggregate(gi, g, mb):
                if mb == 0:
                    for t in range(T):
                        pe.wait_ge(out_ready, T * (gi - 1) + t + 1 + CREDIT)
                        for i in range(3):
                            nc.tensor.matmul(acc1[t], no_nb[:, bass.ds(g * G + t * P, P)], hs3[:, i, :],
                                             start=(i == 0), stop=False)
                pe.wait_ge(prob1_ready, NB * gi + mb + 1)
                for t in range(T):
                    mm = nc.tensor.matmul(acc1[t], prob1[:, mb % 4, t * P:(t + 1) * P], h2[:, mb, :],
                                          start=False, stop=(mb == NB - 1))
                    if mb == NB - 1:
                        mm.then_inc(agg_ready, 1)
                    elif t == T - 1:
                        mm.then_inc(prob1_used, 1)

            with pe.Fori(0, B) as b:
                for g in range(NG):
                    project(NG * b + g, g)
                pe.wait_ge(v_ready, 2 * (NG * b + NG))
                pe.wait_ge(kq_ready, 4 * (NG * b + NG))
                pe.wait_ge(ks_in, 32 * (b + 1))
                attend(NG * b, b, False)
                with pe.Fori(1, NG) as g:
                    attend(NG * b + g, b, True)
                for s in range(SLOTS):
                    tail_step(NG * b + NG - 1, s)
                pe.wait_ge(hs_ready, b + 1)
                hold(pe)
                with pe.Fori(0, NG) as g:
                    for mb in range(NB):
                        aggregate(NG * b + g, g, mb)


def kernel(**inputs):
    import numpy as np
    import concourse.bacc as bacc
    from concourse.bass_utils import run_bass_kernel_spmd

    def t(a):
        return np.ascontiguousarray(np.asarray(a).T)

    p = {k.replace("L0_gnn_", "").replace("L1_gnn_", "L1_"): np.asarray(v) for k, v in inputs.items()}
    B, N, F = p["x"].shape
    host = {
        "x": p["x"], "adj_t": t(p["adj"]),
        "wq_t": t(p["Wq"]), "bq": p["bq"], "wk_t": t(p["Wk"]), "bk": p["bk"], "wv_t": t(p["Wv"]), "bv": p["bv"],
        "wo_t": t(p["Wo"]), "bo": p["bo"], "gamma": p["gamma"], "beta": p["beta"],
        "w1": p["L1_W"], "a1": p["L1_a"].reshape(2, F),
    }
    nc = bacc.Bacc("TRN2", target_bir_lowering=False, num_devices=1, dynamic_dma_scratch_size=1024)
    arrays, args = {}, []
    for name, a in host.items():
        a = np.ascontiguousarray(a)
        arrays[f"in_{name}"] = a
        args.append(nc.dram_tensor(f"in_{name}", a.shape, mybir.dt.from_np(a.dtype), kind="ExternalInput").ap())
    args.append(nc.dram_tensor("out_x", (B, N, F), F32, kind="ExternalOutput").ap())
    gnn_two_layers(nc, *args)
    r = run_bass_kernel_spmd(nc, [arrays], core_ids=[0])
    return r.results[0]["out_x"]
```

```python
from contextlib import ExitStack

import concourse.bass as bass
from concourse import mybir

F32 = mybir.dt.float32
F16 = mybir.dt.float16
BF16 = mybir.dt.bfloat16
U8 = mybir.dt.uint8
I32 = mybir.dt.int32
ALU = mybir.AluOpType
ACT = mybir.ActivationFunctionType
AX_X = mybir.AxisListType.X
RMAX = bass.bass_isa.ReduceOp.max

P = 128
EPS = 1e-5
CLIP = 10.0
EXP_HI = 22026.465794806718
EXP_LO = 4.5399929762484854e-05
SLOPE = 0.2
R_CAP = 100.0
CREDIT = 16


def gnn_two_layers(nc, x, adj_t, wq_t, bq, wk_t, bk, wv_t, bv, wo_t, bo, gamma, beta, w1, a1, out):
    B, N, F = x.shape
    G = 512
    T = G // P
    NG = N // G
    NB = N // P
    KB = F // P
    DH = 64
    HEADS = F // DH
    PAIRS = HEADS // 2
    CHUNK = 256
    CH = N // CHUNK
    CB = CHUNK // P
    SLOTS = CH * PAIRS
    UNITS = 2 * SLOTS
    HALF = SLOTS // 2
    CHH = CH // 2
    W1C = F + 2
    HC = F + 1

    kq_d = nc.dram_tensor("kq_scratch", (B, 4, F, N), F16, kind="Internal").ap()
    hb_d = nc.dram_tensor("hb_scratch", (B, N, F), F32, kind="Internal").ap()
    xb_d = nc.dram_tensor("xb_scratch", (B, N, F), F32, kind="Internal").ap()
    x1_d = nc.dram_tensor("x1_scratch", (B, N, F), F32, kind="Internal").ap()
    s1_d = nc.dram_tensor("s1_scratch", (B, 1, N), F32, kind="Internal").ap()
    inv_d = nc.dram_tensor("inv_scratch", (B, 2, HEADS, CHH, N), F32, kind="Internal").ap()

    def rows(t, b, g):
        return t[b, bass.ds(g * G, G), :].rearrange("(t p) f -> p t f", p=P)

    with ExitStack() as ctx:
        def sb(name, shape, dt):
            return ctx.enter_context(nc.sbuf_tensor(name, shape, dt))

        def pb(name, shape):
            return ctx.enter_context(nc.psum_tensor(name, shape, F32))

        def sem(name):
            return ctx.enter_context(nc.semaphore(name))

        mask = sb("mask", [P, NB, N], U8)
        no_nb = sb("no_nb", [P, N], BF16)
        wqkv = [sb(f"w_{n}", [P, 2, KB, F], F16) for n in "qkv"]
        w1s = sb("w1s", [P, 2, KB, W1C], F16)
        wo = sb("wo", [P, KB, F], F32)
        bias_qk = sb("bias_qk", [P, 2, KB], F32)
        bv_b = sb("bv_b", [P, F], F32)
        bo_b = sb("bo_b", [P, F], F32)
        gamma_b = sb("gamma_b", [P, F], F32)
        beta_b = sb("beta_b", [P, F], F32)
        ident = sb("ident", [P, P], F32)
        pick = sb("pick", [P, 32 + CHH], F32)
        ones_bf = sb("ones_bf", [P, P], BF16)
        minus_half = sb("minus_half", [P, T], F32)
        exp_lo = sb("exp_lo", [P, 1], F32)
        ks = sb("ks", [P, HEADS, N], F16)
        v = sb("v", [P, NB, F], F32)
        h2 = sb("h2", [P, NB, HC], F32)
        s2c = sb("s2c", [P, NB], F32)
        nums = sb("nums", [P, SLOTS, G], F32)
        xg = [nums[:, 2 * i:2 * i + 2, :].rearrange("p a (t f) -> p (a t) f", f=F) for i in range(2)]
        hg = nums[:, 4:6, :].rearrange("p a (t f) -> p (a t) f", f=F)
        hb_s = nums[:, 6:8, :].rearrange("p a (t f) -> p (a t) f", f=F)
        xb_s = nums[:, 8:10, :].rearrange("p a (t f) -> p (a t) f", f=F)
        ht = nums[:, 10:12, :].rearrange("p a n -> p (a n)").bitcast(F16).rearrange("p (s n) -> p s n", s=2)
        kq_s = nums[:, 12:16, :].rearrange("p a n -> p (a n)").bitcast(F16)\
            .rearrange("p (i k n) -> p i k n", i=4, k=KB)
        ln = sb("ln", [P, 16 * T], F32)
        limit = [sb(f"limit{i}", [P, CB, G], F32) for i in range(3)]
        qs = sb("qs", [P, 2, HEADS, G], F16)
        probs = sb("probs", [P, 4, CB * G], F32)
        presum = sb("presum", [P, 4, G], F32)
        inv_den = sb("inv_den", [P, G], F32)
        inv_b = sb("inv_b", [P, PAIRS, CHH, G], F32)
        acc = sb("acc", [P, PAIRS, G], F32)
        ctx_t = sb("ctx_t", [P, PAIRS, G], F32)
        tg = sb("tg", [P, T, F], F32)
        xbg = sb("xbg", [P, T, F], F32)
        x1g = sb("x1g", [P, T, F], F32)
        h1t = sb("h1t", [P, 2, KB, G], F16)
        s1row = sb("s1row", [1, G], F32)
        lt = sb("lt", [P, 16 * T], F32)
        mx = sb("mx", [P, 2], F32)
        s2m = sb("s2m", [P, NB], F32)
        b12 = sb("b12", [P, 2, NB], F32)
        hs, hs_r = (x1g[:, :, :].rearrange("p t f -> p (t f)")[:, i * HC:(i + 1) * HC] for i in range(2))
        hs3 = sb("hs3", [P, 3, HC], BF16)
        x1t = inv_b[:, 0, 0:2, :].rearrange("p a (t f) -> p (a t) f", f=F)
        og = inv_b[:, 0, 2:4, :].rearrange("p a (t f) -> p (a t) f", f=F)
        rden = sb("rden", [P, T], F32)
        rvec = probs[:, 2:4, :].rearrange("p a n -> p (a n)")
        prob1 = probs[:, 0:2, :].rearrange("p a (c n) -> p (a c) n", c=CB)
        scaled = presum

        ps_s = [pb(f"ps_s{i}", [P, CB * G]) for i in range(2)]
        ps_n = [pb(f"ps_n{i}", [P, G]) for i in range(2)]
        ps_d = pb("ps_d", [P, G])
        ps_x = pb("ps_x", [P, G])
        acc1 = [ps_s[t // 2][:, G * (t % 2):G * (t % 2) + HC] for t in range(T)]

        const_in = sem("const_in")
        wst_in = [sem(f"wst_in{i}") for i in range(2)]
        wst_used = sem("wst_used")
        adj_in = [sem(f"adj_in{i}") for i in range(2)]
        adj_used = sem("adj_used")
        pool_set = sem("pool_set")
        mask_bf_ready = sem("mask_bf_ready")
        count_done = sem("count_done")
        setup_done = sem("setup_done")
        step = sem("step")
        x_in = [sem(f"x_in{i}") for i in range(2)]
        var_a = sem("var_a")
        inv_a = sem("inv_a")
        stats_a = sem("stats_a")
        h_ready = sem("h_ready")
        hbxb_ready = sem("hbxb_ready")
        hbxb_out = sem("hbxb_out")
        h_turned = sem("h_turned")
        ht_hi = sem("ht_hi")
        ht_ready = sem("ht_ready")
        proj_ready = sem("proj_ready")
        kq_hi = sem("kq_hi")
        kq_ready = sem("kq_ready")
        kq_out = sem("kq_out")
        v_ready = sem("v_ready")
        ks_in = sem("ks_in")
        q_in = [sem(f"q_in{i}") for i in range(PAIRS)]
        limit_ready = sem("limit_ready")
        scores_ready = sem("scores_ready")
        exp_ready = sem("exp_ready")
        probs_ready = sem("probs_ready")
        presum_ready = sem("presum_ready")
        num_ready = sem("num_ready")
        den_sum = sem("den_sum")
        num_taken = sem("num_taken")
        inv_ready = sem("inv_ready")
        inv_out = sem("inv_out")
        inv_in = sem("inv_in")
        divided = sem("divided")
        normed = sem("normed")
        tail_in = sem("tail_in")
        tail_mm = sem("tail_mm")
        tail_taken = sem("tail_taken")
        var_t = sem("var_t")
        inv_t = sem("inv_t")
        centred = sem("centred")
        x1_ready = sem("x1_ready")
        x1_out = sem("x1_out")
        var_u = sem("var_u")
        inv_u = sem("inv_u")
        stats_u = sem("stats_u")
        h1_ready = sem("h1_ready")
        h1t_hi = sem("h1t_hi")
        s1_out = sem("s1_out")
        s2_max = sem("s2_max")
        s2_all = sem("s2_all")
        s2m_ready = sem("s2m_ready")
        b12_ready = sem("b12_ready")
        s1_in = sem("s1_in")
        s1_cap = sem("s1_cap")
        r_ready = sem("r_ready")
        hs_ready = sem("hs_ready")
        scaled_ready = sem("scaled_ready")
        prob1_ready = sem("prob1_ready")
        prob1_used = sem("prob1_used")
        agg_ready = sem("agg_ready")
        x1_in = sem("x1_in")
        out_ready = sem("out_ready")
        out_done = sem("out_done")

        chain_a, chain_t, chain_u, chain_d, chain_s = (sem(f"chain_{x}") for x in "atuds")
        counted = [
            chain_a, chain_t, chain_u, chain_d, chain_s, *x_in, var_a, inv_a, stats_a, h_ready, hbxb_ready, hbxb_out,
            h_turned, ht_hi, ht_ready, proj_ready, kq_hi, kq_ready, kq_out, v_ready, ks_in, *q_in, limit_ready,
            scores_ready, exp_ready, probs_ready, presum_ready, num_ready, num_taken, den_sum, inv_ready, inv_out, inv_in,
            divided, normed, tail_in, tail_mm, tail_taken, var_t, inv_t, centred, x1_ready, x1_out, var_u, inv_u,
            stats_u, h1_ready, h1t_hi, s1_out, s2_max, s2_all, s2m_ready, b12_ready, s1_in, s1_cap, r_ready,
            hs_ready, scaled_ready, prob1_ready, prob1_used, agg_ready, x1_in, out_ready, out_done,
        ]

        block = ctx.enter_context(nc.Block())

        def hold(eng):
            eng.nop(nofuse=True)

        wst = [xg[0][:, 0:KB, :], xg[1][:, 0:KB, :]]
        a1_b = [hg[:, i, :] for i in range(2)]
        adj_st = [probs[:, 2 * i:2 * i + 2, :].rearrange("p a n -> p (a n)").bitcast(I32) for i in range(2)]
        mask_bf = [presum[:, 2 * i:2 * i + 2, :].rearrange("p a n -> p (a n)").bitcast(BF16) for i in range(2)]

        @block.sync
        def _(sp):
            for s in counted:
                sp.sem_inc(s, CREDIT)

            def load_const(dst, src):
                sp.dma_start(dst, src).then_inc(const_in, 16)

            load_const(wo[:, :, :], wo_t.rearrange("(k p) o -> p k o", p=P))
            for i, t in enumerate((bq, bk)):
                with nc.allow_non_contiguous_dma(reason="one small column per partition"):
                    load_const(bias_qk[:, i, :], t.rearrange("(k p) -> p k", p=P))
            for dst, t in ((bv_b, bv), (bo_b, bo), (gamma_b, gamma), (beta_b, beta)):
                load_const(dst[:, :], t.rearrange("(a f) -> a f", a=1).to_broadcast([P, F]))
            for i in range(2):
                load_const(a1_b[i], a1[i:i + 1, :].to_broadcast([P, F]))
            for i, w in enumerate((wq_t, wk_t, wv_t, w1)):
                if i >= 2:
                    sp.wait_ge(wst_used, i - 1)
                sp.dma_start(wst[i % 2], w.rearrange("(k p) o -> p k o", p=P)).then_inc(wst_in[i % 2], 16)
            for c in range(NB):
                if c >= 2:
                    sp.wait_ge(adj_used, c - 1)
                sp.dma_start(adj_st[c % 2], adj_t[c * P:(c + 1) * P, :]).then_inc(adj_in[c % 2], 16)
            sp.wait_ge(setup_done, 1)

            def load_x(b, g, buf):
                sp.dma_start(xg[buf][:, :, :], rows(x, b, g)).then_inc(x_in[buf], 16)

            def store_projected(b, g, gi):
                sp.wait_ge(hbxb_ready, 2 * gi + 2 + CREDIT)
                hold(sp)
                sp.dma_start(rows(hb_d, b, g), hb_s[:, :, :]).then_inc(hbxb_out, 16)
                sp.dma_start(rows(xb_d, b, g), xb_s[:, :, :]).then_inc(hbxb_out, 16)
                sp.wait_ge(kq_ready, 4 * gi + 4 + CREDIT)
                for i in range(4):
                    sp.dma_start(kq_d[b, i, :, bass.ds(g * G, G)].rearrange("(k p) n -> p k n", p=P),
                                 kq_s[:, i, :, :]).then_inc(kq_out, 16)

            def load_q(b, g, pair):
                for half in range(2):
                    for part in range(2):
                        sp.dma_start(
                            qs[half * DH:(half + 1) * DH, part, 2 * pair:2 * pair + 2, :],
                            kq_d[b, 2 + part, 2 * pair * DH:(2 * pair + 2) * DH, bass.ds(g * G, G)]
                            .rearrange("(h d) n -> d h n", d=DH)).then_inc(q_in[pair], 16)

            def load_tail(b, g, gi):
                sp.wait_ge(tail_mm, 9 * gi + CREDIT)
                sp.dma_start(tg[:, :, :], rows(hb_d, b, g)).then_inc(tail_in, 16)
                sp.dma_start(xbg[:, :, :], rows(xb_d, b, g)).then_inc(tail_in, 16)

            def store_x1(b, g, gi):
                sp.wait_ge(x1_ready, gi + 1 + CREDIT)
                sp.dma_start(rows(x1_d, b, g), x1g[:, :, :]).then_inc(x1_out, 16)

            def spread(b, g, gi, half):
                sp.wait_ge(inv_ready, 2 * gi + half + 1 + CREDIT)
                for h in range(HEADS):
                    sp.dma_start(inv_d[b, half, h, :, bass.ds(g * G, G)], inv_den[32 * h:32 * h + CHH, :])\
                        .then_inc(inv_out, 16)
                sp.wait_ge(normed, SLOTS * gi + HALF * half + CREDIT)
                sp.wait_ge(inv_out, 64 * (2 * gi + half + 1) + CREDIT)
                hold(sp)
                for h in range(HEADS):
                    sp.dma_start(inv_b[h % 2 * DH:(h % 2 + 1) * DH, h // 2, :, :],
                                 inv_d[b, half, h, :, bass.ds(g * G, G)].unsqueeze(0).to_broadcast([DH, CHH, G]))\
                        .then_inc(inv_in, 16)

            def store_out(b, g, gi):
                sp.wait_ge(out_ready, 4 * gi + 4 + CREDIT)
                sp.dma_start(rows(out, b, g), og[:, :, :]).then_inc(out_done, 16)

            with sp.Fori(0, B) as b:
                load_x(b, 0, 0)
                for g in range(NG):
                    gi = NG * b + g
                    if g + 1 < NG:
                        if g >= 1:
                            sp.wait_ge(hbxb_ready, 2 * gi + CREDIT)
                            hold(sp)
                            sp.wait_ge(h_ready, gi + CREDIT)
                            hold(sp)
                        load_x(b, g + 1, (g + 1) % 2)
                    store_projected(b, g, gi)
                sp.wait_ge(kq_out, 16 * 4 * (NG * b + NG) + CREDIT)
                hold(sp)
                for part in range(2):
                    sp.dma_start(ks[part * DH:(part + 1) * DH, :, :],
                                 kq_d[b, part, :, :].rearrange("(h d) n -> d h n", d=DH)).then_inc(ks_in, 16)
                for pair in range(PAIRS):
                    load_q(b, 0, pair)
                sp.wait_ge(hbxb_out, 32 * (NG * b + NG) + CREDIT)
                sp.wait_ge(out_done, 16 * NG * b + CREDIT)
                hold(sp)
                spread(b, 0, NG * b, 0)

                with sp.Fori(1, NG) as g:
                    gi = NG * b + g
                    for pair in range(PAIRS):
                        sp.wait_ge(scores_ready, UNITS * gi - 2 * (PAIRS - 1 - pair) + CREDIT)
                        load_q(b, g, pair)
                    spread(b, g - 1, gi - 1, 1)
                    load_tail(b, g - 1, gi - 1)
                    spread(b, g, gi, 0)
                    store_x1(b, g - 1, gi - 1)
                gl = NG * b + NG - 1
                spread(b, NG - 1, gl, 1)
                load_tail(b, NG - 1, gl)
                store_x1(b, NG - 1, gl)

                sp.wait_ge(s1_out, 16 * (NG * b + NG) + CREDIT)
                sp.wait_ge(x1_out, 16 * (NG * b + NG) + CREDIT)
                hold(sp)
                sp.dma_start(rvec, s1_d[b, :, :].to_broadcast([P, N])).then_inc(s1_in, 16)
                with sp.Fori(0, NG) as g:
                    gi = NG * b + g
                    sp.wait_ge(out_ready, 4 * gi + CREDIT)
                    sp.dma_start(x1t[:, :, :], rows(x1_d, b, g)).then_inc(x1_in, 16)
                    store_out(b, g, gi)
            sp.wait_ge(out_done, 16 * NG * B + CREDIT)

        def work_views(work):
            return (work[:, 0:6 * T].rearrange("p (t s) -> p t s", t=T), work[:, 6 * T:8 * T].rearrange("p (t s) -> p t s", t=T),
                    work[:, 8 * T:9 * T], work[:, 9 * T:10 * T], work[:, 10 * T:11 * T])

        def variances(dve, src, work, done, chain, n):
            st, mv, var, _, _ = work_views(work)
            for t in range(T):
                last = nc.vector.bn_stats(st[:, t, :], src[:, t, :])
            last.then_inc(chain, 1)
            dve.wait_ge(chain, n + 1 + CREDIT)
            hold(dve)
            for t in range(T):
                last = nc.vector.bn_aggr(mv[:, t, :], st[:, t:t + 1, :])
            last.then_inc(chain, 1)
            dve.wait_ge(chain, n + 2 + CREDIT)
            nc.vector.tensor_scalar(var, mv[:, :, 1], EPS, None, ALU.add).then_inc(done, 1)

        def inverse_deviations(work, done):
            _, _, var, inv, _ = work_views(work)
            nc.gpsimd.tensor_tensor(inv, var, minus_half[:, :], ALU.pow).then_inc(done, 1)

        def shifts(work, done):
            _, mv, _, inv, shift = work_views(work)
            nc.vector.scalar_tensor_tensor(out=shift, in0=mv[:, :, 0], scalar=-1.0, in1=inv,
                                           op0=ALU.mult, op1=ALU.mult).then_inc(done, 1)

        def norm_args(work, t):
            _, _, _, inv, shift = work_views(work)
            return dict(scale=inv[:, t:t + 1], bias=shift[:, t:t + 1])

        @block.gpsimd
        def _(pool):
            nc.gpsimd.memset(ident[:, :], 0.0).then_inc(pool_set, 1)
            pool.wait_ge(pool_set, 1)
            nc.gpsimd.affine_select(out=ident[:, :], in_=ident[:, :], compare_op=ALU.not_equal, fill=1.0,
                                    base=0, pattern=[[-1, P]], channel_multiplier=1).then_inc(pool_set, 1)
            nc.gpsimd.memset(minus_half[:, :], -0.5)
            nc.gpsimd.memset(h2[:, :, F:HC], 1.0).then_inc(pool_set, 1)
            pool.wait_ge(const_in, 16 * 9)
            pool.wait_ge(setup_done, 1)

            def save_residuals(gi, buf, xi):
                pool.wait_ge(var_a, gi + 1 + CREDIT)
                pool.wait_ge(pool_set, 3)
                inverse_deviations(ln, inv_a)
                pool.wait_ge(hbxb_out, 32 * gi + CREDIT)
                pool.wait_ge(x_in[buf], 16 * xi + CREDIT)
                for t in range(T):
                    last = nc.gpsimd.tensor_tensor(xb_s[:, t, :], xg[buf][:, t, :], beta_b[:, :], ALU.add)
                last.then_inc(hbxb_ready, 1)
                pool.wait_ge(h_ready, gi + 1 + CREDIT)
                for t in range(T):
                    last = nc.gpsimd.tensor_tensor(hb_s[:, t, :], hg[:, t, :], bo_b[:, :], ALU.add)
                last.then_inc(hbxb_ready, 1)

            def tail_step(gi, s):
                if s == 7:
                    pool.wait_ge(var_t, gi + 1 + CREDIT)
                    inverse_deviations(lt, inv_t)
                if s == 8:
                    pool.wait_ge(var_u, gi + 1 + CREDIT)
                    inverse_deviations(lt, inv_u)

            def attend(gi, g, tail):
                for s in range(SLOTS):
                    for u in (2 * s, 2 * s + 1):
                        pool.wait_ge(probs_ready, UNITS * gi + u + 1 + CREDIT)
                        pool.wait_ge(den_sum, CH * gi + s // PAIRS + CREDIT)
                        nc.gpsimd.tensor_tensor(presum[:, u % 4, :], probs[:, u % 4, 0:G],
                                                probs[:, u % 4, G:2 * G], ALU.add).then_inc(presum_ready, 1)
                    if tail:
                        tail_step(gi - 1, s)

            with pool.Fori(0, B) as b:
                for g in range(NG):
                    save_residuals(NG * b + g, g % 2, NG // 2 * b + g // 2 + 1)
                attend(NG * b, 0, False)
                with pool.Fori(1, NG) as g:
                    attend(NG * b + g, g, True)
                for s in range(SLOTS):
                    tail_step(NG * b + NG - 1, s)
                pool.wait_ge(s2_max, b + 1 + CREDIT)
                hold(pool)
                nc.gpsimd.partition_all_reduce(mx[:, 1:2], mx[:, 0:1], P, RMAX).then_inc(s2_all, 1)


        @block.vector
        def _(dve):
            steps = [0]

            def link(ins):
                steps[0] += 1
                ins.then_inc(step, 1)
                dve.wait_ge(step, steps[0])

            link(nc.vector.memset(pick[:, :], 0.0))
            link(nc.vector.memset(pick[:, CHH - 1::CHH], 1.0))
            nc.vector.memset(exp_lo[:, :], EXP_LO)
            link(nc.vector.memset(ones_bf[:, :], 1.0))
            dve.wait_ge(const_in, 16 * 9)
            for i in range(4):
                dve.wait_ge(wst_in[i % 2], 16 * (i // 2 + 1))
                if i < 3:
                    dst, src = wqkv[i], wst[i % 2]
                else:
                    ext = tg[:, 0:3, :].rearrange("p t f -> p (t f)")[:, 0:KB * W1C].rearrange("p (k c) -> p k c", k=KB)
                    prod = x1g[:, 0:2 * KB, :]
                    for k in range(KB):
                        nc.vector.tensor_copy(ext[:, k, 0:F], wst[1][:, k, :])
                        for j in range(2):
                            last = nc.vector.tensor_tensor(prod[:, 2 * k + j, :], wst[1][:, k, :], a1_b[j], ALU.mult)
                    link(last)
                    for k in range(KB):
                        last = nc.vector.tensor_reduce(ext[:, k, F:F + 2], prod[:, 2 * k:2 * k + 2, :], AX_X, ALU.add)
                    link(last)
                    dst, src = w1s, ext
                link(nc.vector.tensor_copy(dst[:, 0, :, :], src))
                steps[0] += 1
                nc.vector.tensor_tensor(dst[:, 1, :, :], src, dst[:, 0, :, :], ALU.subtract).then_inc(step, 1)
                dve.wait_ge(step, steps[0])
                dve.sem_inc(wst_used, 1)
            for c in range(NB):
                dve.wait_ge(adj_in[c % 2], 16 * (c // 2 + 1))
                nc.vector.tensor_scalar(mask[:, c, :], adj_st[c % 2], 0, None, ALU.not_equal).then_inc(adj_used, 1)
                dve.wait_ge(adj_used, c + 1)
                if c >= 2:
                    dve.wait_ge(count_done, c - 1)
                nc.vector.tensor_copy(mask_bf[c % 2], mask[:, c, :]).then_inc(mask_bf_ready, 1)
            dve.wait_ge(count_done, NB)
            for i in range(2):
                last = nc.vector.tensor_scalar(no_nb[:, i * CB * G:(i + 1) * CB * G], ps_s[i][:, :], 0.5, None, ALU.is_lt)
                if i == 1:
                    last.then_inc(setup_done, 1)
                else:
                    link(last)

            def project(b, g, gi, buf, xi):
                dve.wait_ge(x_in[buf], 16 * xi + CREDIT)
                dve.wait_ge(h_ready, gi + CREDIT)
                variances(dve, xg[buf], ln, var_a, chain_a, 2 * gi)
                dve.wait_ge(inv_a, gi + 1 + CREDIT)
                shifts(ln, stats_a)
                dve.wait_ge(ht_hi, gi + 1 + CREDIT)
                nc.vector.tensor_tensor(ht[:, 1, :], ps_s[0][:, :], ht[:, 0, :], ALU.subtract).then_inc(ht_ready, 1)
                dve.wait_ge(kq_out, 64 * gi + CREDIT)
                for i, ps in enumerate((ps_n[0][:, :], ps_n[1][:, :], ps_s[1][:, 0:G], ps_s[1][:, G:2 * G])):
                    dve.wait_ge(kq_hi, 4 * gi + i + 1 + CREDIT)
                    w, k = 1 - i // 2, i % 2
                    nc.vector.scalar_tensor_tensor(
                        out=kq_s[:, 2 * (i // 2) + 1, k, :], in0=ps, scalar=bias_qk[:, w, k:k + 1],
                        in1=kq_s[:, 2 * (i // 2), k, :], op0=ALU.add, op1=ALU.subtract).then_inc(kq_ready, 1)
                for i, ps in enumerate((ps_d, ps_x)):
                    dve.wait_ge(proj_ready, 6 * gi + 5 + i + CREDIT)
                    for t in range(2):
                        last = nc.vector.tensor_tensor(v[:, bass.ds(T * g + 2 * i + t, 1), :],
                                                       ps[:, t * F:(t + 1) * F].unsqueeze(1),
                                                       bv_b[:, :].unsqueeze(1), ALU.add)
                    last.then_inc(v_ready, 1)

            def bound(gi, u):
                dve.wait_ge(exp_ready, UNITS * gi + u + 1 + CREDIT)
                if u % HEADS == 0:
                    dve.wait_ge(limit_ready, CH * gi + u // HEADS + 1 + CREDIT)
                dve.wait_ge(presum_ready, UNITS * gi + max(u - 3, 0) + CREDIT)
                dve.wait_ge(num_ready, SLOTS * gi + max(u // 2 - 1, 0) + CREDIT)
                nc.vector.scalar_tensor_tensor(
                    out=probs[:, u % 4, :], in0=ps_s[u % 2][:, :], scalar=EXP_LO,
                    in1=limit[u // HEADS % 3][:, :, :].rearrange("p c n -> p (c n)"),
                    op0=ALU.max, op1=ALU.min).then_inc(probs_ready, 1)

            def invert(gi, half):
                dve.wait_ge(inv_out, 64 * (2 * gi + half) + CREDIT)
                dve.wait_ge(den_sum, CH * gi + CHH * (half + 1) + CREDIT)
                nc.vector.reciprocal(inv_den[:, :], ps_d[:, :]).then_inc(inv_ready, 1)

            def divide(gi, s):
                c, p = s // PAIRS, s % PAIRS
                dve.wait_ge(inv_in, 64 * (2 * gi + c // CHH + 1) + CREDIT)
                dve.wait_ge(num_taken, SLOTS * gi + s + 1 + CREDIT)
                dve.wait_ge(normed, SLOTS * gi + s - 1 + CREDIT)
                if c == 0:
                    nc.vector.tensor_tensor(acc[:, p, :], nums[:, s, :], inv_b[:, p, c % CHH, :], ALU.mult)\
                        .then_inc(normed, 1)
                    return
                nc.vector.tensor_tensor(nums[:, s, :], nums[:, s, :], inv_b[:, p, c % CHH, :], ALU.mult)\
                    .then_inc(divided, 1)
                dve.wait_ge(divided, (SLOTS - PAIRS) * gi + s - PAIRS + 1 + CREDIT)
                dst = ctx_t if c == CH - 1 else acc
                nc.vector.tensor_tensor(dst[:, p, :], acc[:, p, :], nums[:, s, :], ALU.add).then_inc(normed, 1)

            def tail_add(gi, a):
                if a == 0:
                    dve.wait_ge(tail_in, 32 * gi + 32 + CREDIT)
                dve.wait_ge(tail_mm, 9 * gi + a + 1 + CREDIT)
                nc.vector.tensor_tensor(tg[:, 2 * a:2 * a + 2, :],
                                        ps_x[:, :].rearrange("p (t f) -> p t f", t=2),
                                        tg[:, 2 * a:2 * a + 2, :], ALU.add).then_inc(tail_taken, 1)

            def tail_var(gi):
                dve.wait_ge(tail_taken, 9 * gi + 2 + CREDIT)
                variances(dve, tg, lt, var_t, chain_t, 2 * gi)

            def tail_x1(gi):
                dve.wait_ge(inv_t, gi + 1 + CREDIT)
                dve.wait_ge(x1_out, 16 * gi + CREDIT)
                _, mv, _, inv, _ = work_views(lt)
                for t in range(T):
                    last = nc.vector.scalar_tensor_tensor(out=tg[:, t, :], in0=tg[:, t, :], scalar=mv[:, t, 0:1],
                                                          in1=gamma_b[:, :], op0=ALU.subtract, op1=ALU.mult)
                last.then_inc(centred, 1)
                dve.wait_ge(centred, gi + 1 + CREDIT)
                for t in range(T):
                    last = nc.vector.scalar_tensor_tensor(out=x1g[:, t, :], in0=tg[:, t, :], scalar=inv[:, t:t + 1],
                                                          in1=xbg[:, t, :], op0=ALU.mult, op1=ALU.add)
                last.then_inc(x1_ready, 1)
                dve.wait_ge(x1_ready, gi + 1 + CREDIT)
                variances(dve, x1g, lt, var_u, chain_u, 2 * gi)

            def tail_low(gi, k):
                dve.wait_ge(h1t_hi, KB * gi + k + 1 + CREDIT)
                nc.vector.tensor_tensor(h1t[:, 1, k, :], ps_x[:, :], h1t[:, 0, k, :], ALU.subtract)\
                    .then_inc(tail_taken, 1)

            def attend(gi, prev):
                for u in range(2):
                    bound(gi, u)
                for s in range(SLOTS):
                    if s + 1 < SLOTS:
                        bound(gi, 2 * s + 2)
                        bound(gi, 2 * s + 3)
                    if prev:
                        finish_step(gi - 1, s)
                    if s == HALF:
                        invert(gi, 0)
                    if s > HALF:
                        divide(gi, s - HALF - 1)
                divide(gi, HALF - 1)

            def finish_step(gi, s):
                if s == 0:
                    invert(gi, 1)
                if 1 <= s <= 4:
                    divide(gi, HALF + 2 * s - 2)
                    divide(gi, HALF + 2 * s - 1)
                if s == 6:
                    tail_add(gi, 0)
                if s == 7:
                    tail_add(gi, 1)
                    tail_var(gi)
                if s == 8:
                    tail_x1(gi)
                if s == 9:
                    dve.wait_ge(inv_u, gi + 1 + CREDIT)
                    shifts(lt, stats_u)
                if s in (12, 13):
                    tail_low(gi, s - 12)

            def aggregate(gi, mb):
                dve.wait_ge(scaled_ready, NB * gi + mb + 1 + CREDIT)
                if mb == 3:
                    dve.wait_ge(agg_ready, T * gi + CREDIT)
                else:
                    dve.wait_ge(prob1_used, (NB - 1) * gi + (mb - 2 if mb < 3 else mb - 3) + CREDIT)
                nc.vector.scalar_tensor_tensor(
                    out=prob1[:, mb % 4, :], in0=scaled[:, mb % 4, :], scalar=b12[:, 1, mb:mb + 1],
                    in1=mask[:, mb, bass.ds(self_g[0] * G, G)], op0=ALU.max, op1=ALU.mult).then_inc(prob1_ready, 1)

            self_g = [0]

            def emit(gi):
                dve.wait_ge(x1_in, 16 * (gi + 1) + CREDIT)
                dve.wait_ge(out_done, 16 * gi + CREDIT)
                for t in range(T):
                    dve.wait_ge(agg_ready, T * gi + t + 1 + CREDIT)
                    dve.wait_ge(out_ready, T * gi + t + CREDIT)
                    nc.vector.reciprocal(rden[:, t:t + 1], acc1[t][:, F:HC]).then_inc(chain_d, 1)
                    dve.wait_ge(chain_d, T * gi + t + 1 + CREDIT)
                    nc.vector.scalar_tensor_tensor(out=og[:, t, :], in0=acc1[t][:, 0:F], scalar=rden[:, t:t + 1],
                                                   in1=x1t[:, t, :], op0=ALU.mult, op1=ALU.add).then_inc(out_ready, 1)

            S_LINKS = 5
            with dve.Fori(0, B) as b:
                for g in range(NG):
                    project(b, g, NG * b + g, g % 2, NG // 2 * b + g // 2 + 1)
                attend(NG * b, False)
                with dve.Fori(1, NG) as g:
                    attend(NG * b + g, True)
                gl = NG * b + NG - 1
                for s in range(SLOTS):
                    finish_step(gl, s)

                dve.wait_ge(tail_taken, 9 * gl + 9 + CREDIT)
                nc.vector.tensor_reduce(mx[:, 0:1], s2c[:, :], AX_X, ALU.max).then_inc(s2_max, 1)
                n = [0]

                def link_b(ins):
                    n[0] += 1
                    ins.then_inc(chain_s, 1)
                    dve.wait_ge(chain_s, S_LINKS * b + n[0] + CREDIT)

                dve.wait_ge(x1_out, 16 * NG * (b + 1) + CREDIT)
                link_b(nc.vector.tensor_reduce(hs[:, :], h2[:, :, :].rearrange("p m f -> p f m"), AX_X, ALU.add))
                link_b(nc.vector.tensor_copy(hs3[:, 0, :], hs[:, :]))
                link_b(nc.vector.tensor_tensor(hs_r[:, :], hs[:, :], hs3[:, 0, :], ALU.subtract))
                link_b(nc.vector.tensor_copy(hs3[:, 1, :], hs_r[:, :]))
                link_b(nc.vector.tensor_tensor(hs[:, :], hs_r[:, :], hs3[:, 1, :], ALU.subtract))
                nc.vector.tensor_copy(hs3[:, 2, :], hs[:, :]).then_inc(hs_ready, 1)
                dve.wait_ge(s2_all, b + 1 + CREDIT)
                nc.vector.tensor_scalar(s2m[:, :], s2c[:, :], mx[:, 1:2], None, ALU.subtract).then_inc(s2m_ready, 1)
                dve.wait_ge(s1_in, 16 * (b + 1) + CREDIT)
                nc.vector.tensor_scalar(rvec, rvec, mx[:, 1:2], R_CAP, ALU.add, ALU.min).then_inc(s1_cap, 1)
                dve.wait_ge(b12_ready, 2 * b + 2 + CREDIT)

                self_g[0] = 0
                for mb in range(NB):
                    aggregate(NG * b, mb)
                with dve.Fori(1, NG) as g:
                    self_g[0] = g
                    for mb in range(NB):
                        aggregate(NG * b + g, mb)
                        if mb == 2:
                            emit(NG * b + g - 1)
                emit(gl)

        @block.scalar
        def _(act):
            def project(gi, buf):
                act.wait_ge(stats_a, gi + 1 + CREDIT)
                act.wait_ge(h_turned, gi + CREDIT)
                act.wait_ge(hbxb_ready, 2 * gi + CREDIT)
                for t in range(T):
                    last = nc.scalar.activation(hg[:, t, :], xg[buf][:, t, :], ACT.Relu,
                                                **norm_args(ln, t))
                last.then_inc(h_ready, 1)
                act.wait_ge(h_turned, gi + 1 + CREDIT)
                act.wait_ge(proj_ready, 6 * gi + CREDIT)
                nc.scalar.copy(ht[:, 0, :], ps_s[0][:, :]).then_inc(ht_hi, 1)
                act.wait_ge(kq_out, 64 * gi + CREDIT)
                for i, ps in enumerate((ps_n[0][:, :], ps_n[1][:, :], ps_s[1][:, 0:G], ps_s[1][:, G:2 * G])):
                    act.wait_ge(proj_ready, 6 * gi + i + 1 + CREDIT)
                    w, k = 1 - i // 2, i % 2
                    nc.scalar.activation(kq_s[:, 2 * (i // 2), k, :], ps, ACT.Identity,
                                         bias=bias_qk[:, w, k:k + 1]).then_inc(kq_hi, 1)

            cur_b = [0]

            def exp(gi, u):
                act.wait_ge(scores_ready, UNITS * gi + u + 1 + CREDIT)
                nc.scalar.activation(ps_s[u % 2][:, :], ps_s[u % 2][:, :], ACT.Exp, scale=DH ** -0.5).then_inc(exp_ready, 1)

            def take_num(gi, s):
                act.wait_ge(num_ready, SLOTS * gi + s + 1 + CREDIT)
                act.wait_ge(normed, SLOTS * (gi - 1) + s + 1 + CREDIT)
                nc.scalar.copy(nums[:, s, :], ps_n[s % 2][:, :]).then_inc(num_taken, 1)

            def rectify(gi):
                act.wait_ge(stats_u, gi + 1 + CREDIT)
                for t in range(T):
                    last = nc.scalar.activation(tg[:, t, :], x1g[:, t, :], ACT.Relu,
                                                **norm_args(lt, t))
                last.then_inc(h1_ready, 1)

            def tail_high(gi, k):
                act.wait_ge(tail_mm, 9 * gi + 3 + k + CREDIT)
                nc.scalar.copy(h1t[:, 0, k, :], ps_x[:, :]).then_inc(h1t_hi, 1)

            def take_features(gi, g, t):
                act.wait_ge(tail_mm, 9 * gi + 5 + t + CREDIT)
                hold(act)
                nc.scalar.copy(h2[:, bass.ds(T * g + t, 1), 0:F], ps_x[:, 0:F].unsqueeze(1))
                nc.scalar.copy(s2c[:, bass.ds(T * g + t, 1)], ps_x[:, F + 1:F + 2]).then_inc(tail_taken, 1)

            def take_s1(gi, g):
                act.wait_ge(tail_mm, 9 * gi + 9 + CREDIT)
                act.wait_ge(s1_out, 16 * gi + CREDIT)
                nc.scalar.copy(s1row[:, :], ps_x[0:1, :]).then_inc(tail_taken, 1)
                act.wait_ge(tail_taken, 9 * gi + 9 + CREDIT)
                act.dma_start(s1_d[cur_b[0], :, bass.ds(g * G, G)], s1row[:, :]).then_inc(s1_out, 16)

            def tail_step(gi, g, s):
                if s == 10:
                    rectify(gi)
                if s in (11, 12):
                    tail_high(gi, s - 11)
                if s in (14, 15):
                    take_features(gi, g, 2 * s - 28)
                    take_features(gi, g, 2 * s - 27)
                if s == 15:
                    take_s1(gi, g)

            def expand(gi, g, c):
                act.wait_ge(probs_ready, UNITS * gi + (HEADS * (c - 2) if c >= 3 else 0) + CREDIT)
                hold(act)
                nc.scalar.activation(limit[c % 3][:, :, :], mask[:, CB * c:CB * c + CB, bass.ds(g * G, G)],
                                     ACT.Identity, scale=EXP_HI - EXP_LO, bias=exp_lo[:, :]).then_inc(limit_ready, 1)

            def attend(gi, g, tail):
                for c in range(2):
                    expand(gi, g, c)
                for u in range(2):
                    exp(gi, u)
                for s in range(SLOTS):
                    if s + 1 < SLOTS:
                        exp(gi, 2 * s + 2)
                        exp(gi, 2 * s + 3)
                    take_num(gi, s)
                    if s % 2 == 0 and s // 2 + 2 < CH:
                        expand(gi, g, s // 2 + 2)
                    if tail:
                        tail_step(gi - 1, g - 1, s)

            def scale(gi, g, mb):
                act.wait_ge(prob1_ready, NB * gi + max(mb - 3, 0) + CREDIT)
                hold(act)
                nc.scalar.activation(scaled[:, mb % 4, :], rvec[:, bass.ds(g * G, G)], ACT.Copy,
                                     scale=b12[:, 0, mb:mb + 1]).then_inc(scaled_ready, 1)

            act.wait_ge(setup_done, 1)
            with act.Fori(0, B) as b:
                cur_b[0] = b
                for g in range(NG):
                    project(NG * b + g, g % 2)
                act.wait_ge(hbxb_out, 32 * (NG * b + NG) + CREDIT)
                attend(NG * b, 0, False)
                with act.Fori(1, NG) as g:
                    attend(NG * b + g, g, True)
                for s in range(SLOTS):
                    tail_step(NG * b + NG - 1, NG - 1, s)
                act.wait_ge(s2m_ready, b + 1 + CREDIT)
                nc.scalar.activation(b12[:, 0, :], s2m[:, :], ACT.Exp).then_inc(b12_ready, 1)
                nc.scalar.activation(b12[:, 1, :], s2m[:, :], ACT.Exp, scale=SLOPE).then_inc(b12_ready, 1)
                act.wait_ge(s1_cap, b + 1 + CREDIT)
                nc.scalar.activation(rvec, rvec, ACT.Exp, scale=1.0 - SLOPE).then_inc(r_ready, 1)
                act.wait_ge(b12_ready, 2 * b + 2 + CREDIT)
                act.wait_ge(r_ready, b + 1 + CREDIT)
                with act.Fori(0, NG) as g:
                    for mb in range(NB):
                        scale(NG * b + g, g, mb)

        @block.tensor
        def _(pe):
            PARTS = ((0, 0), (0, 1), (1, 0))

            pe.wait_ge(step, 1)
            for c in range(NB):
                pe.wait_ge(mask_bf_ready, c + 1)
                for g in range(NG):
                    mm = nc.tensor.matmul(ps_s[g // 2][:, G * (g % 2):G * (g % 2) + G], ones_bf[:, :],
                                          mask_bf[c % 2][:, 0:N][:, g * G:(g + 1) * G],
                                          start=(c == 0), stop=(c == NB - 1))
                mm.then_inc(count_done, 1)
            pe.wait_ge(pool_set, 3)
            pe.wait_ge(setup_done, 1)

            def project(gi, t0):
                pe.wait_ge(h_ready, gi + 1 + CREDIT)
                for k in range(KB):
                    for t in range(T):
                        mm = nc.tensor.transpose(ps_s[0][:, k * G + t * P:k * G + (t + 1) * P],
                                                 hg[:, t, k * P:(k + 1) * P], ident[:, :])
                mm.then_inc(h_turned, 1)
                pe.wait_ge(ht_ready, gi + 1 + CREDIT)
                pe.wait_ge(kq_ready, 4 * gi + CREDIT)
                for i, ps in enumerate((ps_n[0][:, :], ps_n[1][:, :], ps_s[1][:, 0:G], ps_s[1][:, G:2 * G])):
                    w, fb = wqkv[1 - i // 2], i % 2
                    n = 0
                    for k in range(KB):
                        for a, c in PARTS:
                            mm = nc.tensor.matmul(ps, w[:, a, k, fb * P:(fb + 1) * P], ht[:, c, k * G:(k + 1) * G],
                                                  start=(n == 0), stop=(n == 3 * KB - 1))
                            n += 1
                    mm.then_inc(proj_ready, 1)
                pe.wait_ge(v_ready, 2 * gi + CREDIT)
                for i, ps in enumerate((ps_d, ps_x)):
                    for t in range(2):
                        n = 0
                        for k in range(KB):
                            for a, c in PARTS:
                                at = k * G + (2 * i + t) * P
                                mm = nc.tensor.matmul(ps[:, t * F:(t + 1) * F], ht[:, a, at:at + P], wqkv[2][:, c, k, :],
                                                      start=(n == 0), stop=(n == 3 * KB - 1))
                                n += 1
                    mm.then_inc(proj_ready, 1)

            def score(gi, b, u):
                h, c = u % HEADS, u // HEADS
                if c == 0 and h % 2 == 0:
                    pe.wait_ge(q_in[h // 2], 64 * (gi + 1) + CREDIT)
                pe.wait_ge(probs_ready, UNITS * gi + u - 1 + CREDIT)
                for cb in range(CB):
                    for part in range(2):
                        mm = nc.tensor.matmul(ps_s[u % 2][:, cb * G:(cb + 1) * G],
                                              ks[:, h, (CB * c + cb) * P:(CB * c + cb + 1) * P],
                                              qs[:, part, h, :], start=(part == 0), stop=(part == 1))
                mm.then_inc(scores_ready, 1)

            def context(gi, s):
                c, p = s // PAIRS, s % PAIRS
                pe.wait_ge(probs_ready, UNITS * gi + 2 * s + 2 + CREDIT)
                pe.wait_ge(num_taken, SLOTS * gi + s - 1 + CREDIT)
                for cb in range(CB):
                    for h in range(2):
                        mm = nc.tensor.matmul(ps_n[s % 2][h * DH:(h + 1) * DH, :],
                                              v[:, CB * c + cb, (2 * p + h) * DH:(2 * p + h + 1) * DH],
                                              probs[:, (2 * s + h) % 4, cb * G:(cb + 1) * G],
                                              start=(cb == 0), stop=(cb == CB - 1))
                mm.then_inc(num_ready, 1)

            def denominator(gi, c):
                pe.wait_ge(presum_ready, UNITS * gi + HEADS * (c + 1) + CREDIT)
                if c % CHH == 0:
                    pe.wait_ge(inv_ready, 2 * gi + c // CHH + CREDIT)
                for h in range(HEADS):
                    mm = nc.tensor.matmul(ps_d[32 * h:32 * (h + 1), :], pick[:, CHH - 1 - c % CHH:CHH + 31 - c % CHH],
                                          presum[:, h, :], start=(c % CHH == 0), stop=(c % CHH == CHH - 1),
                                          tile_position=(0, 32 * h))
                mm.then_inc(den_sum, 1)

            def tail_out(gi, a):
                if a == 0:
                    pe.wait_ge(normed, SLOTS * (gi + 1) + CREDIT)
                pe.wait_ge(tail_taken, 9 * gi + a + CREDIT)
                for t in range(2):
                    for k in range(KB):
                        at = (2 * a + t) * P
                        mm = nc.tensor.matmul(ps_x[:, t * F:(t + 1) * F], ctx_t[:, k, at:at + P], wo[:, k, :],
                                              start=(k == 0), stop=(k == KB - 1))
                mm.then_inc(tail_mm, 1)

            def tail_turn(gi, k):
                if k == 0:
                    pe.wait_ge(h1_ready, gi + 1 + CREDIT)
                pe.wait_ge(tail_taken, 9 * gi + 2 + k + CREDIT)
                for t in range(T):
                    mm = nc.tensor.transpose(ps_x[:, t * P:(t + 1) * P], tg[:, t, k * P:(k + 1) * P], ident[:, :])
                mm.then_inc(tail_mm, 1)

            def tail_features(gi, t):
                pe.wait_ge(tail_taken, 9 * gi + 4 + t + CREDIT)
                n = 0
                for k in range(KB):
                    for a, c in PARTS:
                        mm = nc.tensor.matmul(ps_x[:, 0:W1C], h1t[:, a, k, t * P:(t + 1) * P], w1s[:, c, k, :],
                                              start=(n == 0), stop=(n == 3 * KB - 1))
                        n += 1
                mm.then_inc(tail_mm, 1)

            def tail_s1(gi):
                pe.wait_ge(tail_taken, 9 * gi + 8 + CREDIT)
                n = 0
                for k in range(KB):
                    for a, c in PARTS:
                        mm = nc.tensor.matmul(ps_x[0:1, :], w1s[:, a, k, F:F + 1], h1t[:, c, k, :],
                                              start=(n == 0), stop=(n == 3 * KB - 1))
                        n += 1
                mm.then_inc(tail_mm, 1)

            def tail_step(gi, s):
                if s in (5, 6):
                    tail_out(gi, s - 5)
                if s in (11, 12):
                    tail_turn(gi, s - 11)
                if s in (14, 15):
                    tail_features(gi, 2 * s - 28)
                    tail_features(gi, 2 * s - 27)
                if s == 15:
                    tail_s1(gi)

            def attend(gi, b, tail):
                for u in range(2):
                    score(gi, b, u)
                for s in range(SLOTS):
                    if s + 1 < SLOTS:
                        score(gi, b, 2 * s + 2)
                        score(gi, b, 2 * s + 3)
                    context(gi, s)
                    if s % PAIRS == PAIRS - 1:
                        denominator(gi, s // PAIRS)
                    if tail:
                        tail_step(gi - 1, s)

            def aggregate(gi, g, mb):
                if mb == 0:
                    for t in range(T):
                        pe.wait_ge(out_ready, T * (gi - 1) + t + 1 + CREDIT)
                        for i in range(3):
                            nc.tensor.matmul(acc1[t], no_nb[:, bass.ds(g * G + t * P, P)], hs3[:, i, :],
                                             start=(i == 0), stop=False)
                pe.wait_ge(prob1_ready, NB * gi + mb + 1 + CREDIT)
                for t in range(T):
                    mm = nc.tensor.matmul(acc1[t], prob1[:, mb % 4, t * P:(t + 1) * P], h2[:, mb, :],
                                          start=False, stop=(mb == NB - 1))
                    if mb == NB - 1:
                        mm.then_inc(agg_ready, 1)
                    elif t == T - 1:
                        mm.then_inc(prob1_used, 1)

            with pe.Fori(0, B) as b:
                for g in range(NG):
                    project(NG * b + g, g)
                pe.wait_ge(v_ready, 2 * (NG * b + NG) + CREDIT)
                pe.wait_ge(kq_ready, 4 * (NG * b + NG) + CREDIT)
                pe.wait_ge(ks_in, 32 * (b + 1) + CREDIT)
                attend(NG * b, b, False)
                with pe.Fori(1, NG) as g:
                    attend(NG * b + g, b, True)
                for s in range(SLOTS):
                    tail_step(NG * b + NG - 1, s)
                pe.wait_ge(hs_ready, b + 1 + CREDIT)
                hold(pe)
                with pe.Fori(0, NG) as g:
                    for mb in range(NB):
                        aggregate(NG * b + g, g, mb)


def kernel(**inputs):
    import numpy as np
    import concourse.bacc as bacc
    from concourse.bass_utils import run_bass_kernel_spmd

    def t(a):
        return np.ascontiguousarray(np.asarray(a).T)

    p = {k.replace("L0_gnn_", "").replace("L1_gnn_", "L1_"): np.asarray(v) for k, v in inputs.items()}
    B, N, F = p["x"].shape
    host = {
        "x": p["x"], "adj_t": t(p["adj"]),
        "wq_t": t(p["Wq"]), "bq": p["bq"], "wk_t": t(p["Wk"]), "bk": p["bk"], "wv_t": t(p["Wv"]), "bv": p["bv"],
        "wo_t": t(p["Wo"]), "bo": p["bo"], "gamma": p["gamma"], "beta": p["beta"],
        "w1": p["L1_W"], "a1": p["L1_a"].reshape(2, F),
    }
    nc = bacc.Bacc("TRN2", target_bir_lowering=False, num_devices=1, dynamic_dma_scratch_size=1024)
    arrays, args = {}, []
    for name, a in host.items():
        a = np.ascontiguousarray(a)
        arrays[f"in_{name}"] = a
        args.append(nc.dram_tensor(f"in_{name}", a.shape, mybir.dt.from_np(a.dtype), kind="ExternalInput").ap())
    args.append(nc.dram_tensor("out_x", (B, N, F), F32, kind="ExternalOutput").ap())
    gnn_two_layers(nc, *args)
    r = run_bass_kernel_spmd(nc, [arrays], core_ids=[0])
    return r.results[0]["out_x"]
```

```python
from contextlib import ExitStack

import concourse.bass as bass
from concourse import mybir

F32 = mybir.dt.float32
F16 = mybir.dt.float16
BF16 = mybir.dt.bfloat16
U8 = mybir.dt.uint8
I32 = mybir.dt.int32
ALU = mybir.AluOpType
ACT = mybir.ActivationFunctionType
AX_X = mybir.AxisListType.X
RMAX = bass.bass_isa.ReduceOp.max

P = 128
EPS = 1e-5
CLIP = 10.0
EXP_HI = 22026.465794806718
EXP_LO = 4.5399929762484854e-05
SLOPE = 0.2
R_CAP = 100.0
CREDIT = 16


def gnn_two_layers(nc, x, adj_t, wq_t, bq, wk_t, bk, wv_t, bv, wo_t, bo, gamma, beta, w1, a1, out):
    B, N, F = x.shape
    G = 512
    T = G // P
    NG = N // G
    NB = N // P
    KB = F // P
    DH = 64
    HEADS = F // DH
    PAIRS = HEADS // 2
    CHUNK = 256
    CH = N // CHUNK
    CB = CHUNK // P
    SLOTS = CH * PAIRS
    UNITS = 2 * SLOTS
    HALF = SLOTS // 2
    CHH = CH // 2
    PROJ = 6
    W1C = F + 2
    TURNS = 7
    HC = F + 1

    kq_d = nc.dram_tensor("kq_scratch", (B + 1, 4, F, N), F16, kind="Internal").ap()
    x1_d = nc.dram_tensor("x1_scratch", (B, N, F), F32, kind="Internal").ap()
    s1_d = nc.dram_tensor("s1_scratch", (B, NB, P), F32, kind="Internal").ap()
    inv_d = nc.dram_tensor("inv_scratch", (B, NG, 2, P, HEADS * CHH * G // P), F32, kind="Internal").ap()

    def rows(t, b, g):
        return t[b, bass.ds(g * G, G), :].rearrange("(t p) f -> p t f", p=P)

    with ExitStack() as ctx:
        def sb(name, shape, dt):
            return ctx.enter_context(nc.sbuf_tensor(name, shape, dt))

        def pb(name, shape):
            return ctx.enter_context(nc.psum_tensor(name, shape, F32))

        def sem(name):
            return ctx.enter_context(nc.semaphore(name))

        mask = sb("mask", [P, NB, N], U8)
        no_nb = sb("no_nb", [P, N], BF16)
        wqkv = [sb(f"w_{n}", [P, 2, KB, F], F16) for n in "qkv"]
        w1s = sb("w1s", [P, 2, KB, W1C], F16)
        wo = sb("wo", [P, KB, F], F32)
        bias_qk = sb("bias_qk", [P, 2, KB], F32)
        bv_b = sb("bv_b", [P, F], F32)
        bo_b = sb("bo_b", [P, F], F32)
        gamma_b = sb("gamma_b", [P, F], F32)
        beta_b = sb("beta_b", [P, F], F32)
        ident = sb("ident", [P, P], F32)
        pick = sb("pick", [P, 32 + CHH], F32)
        ones_bf = sb("ones_bf", [P, P], BF16)
        minus_half = sb("minus_half", [P, T], F32)
        exp_lo = sb("exp_lo", [P, 1], F32)
        ks = sb("ks", [P, HEADS, N], F16)
        v = sb("v", [P, NB, F], F32)
        h2 = sb("h2", [P, NB, HC], F32)
        nums = sb("nums", [P, SLOTS, G], F32)
        xg = [nums[:, 2 * i:2 * i + 2, :].rearrange("p a (t f) -> p (a t) f", f=F) for i in range(2)]
        hg = nums[:, 4:6, :].rearrange("p a (t f) -> p (a t) f", f=F)
        ln = [sb(f"ln{i}", [P, 11 * T], F32) for i in range(2)]
        kept = sb("kept", [P, NG, 2 * T], F32)
        limits = sb("limits", [P, 3, CB, G], F32)
        limit = [limits[:, i, :, :] for i in range(3)]
        lim_h = limits[:, :, :, :].rearrange("p i c n -> p i (c n)")
        ht = [t.rearrange("p a n -> p (a n)").bitcast(F16).rearrange("p (s n) -> p s n", s=2)
              for t in (lim_h[:, 0:1, :], nums[:, 6:8, :])]
        qs = sb("qs", [P, 2, HEADS, G], F16)
        probs = sb("probs", [P, 4, CB * G], F32)
        kq_s = [t.rearrange("p a n -> p (a n)").bitcast(F16).rearrange("p (i k n) -> p i k n", i=4, k=KB)
                for t in (lim_h[:, 1:3, :], probs[:, 0:2, :], lim_h[:, 1:3, :], nums[:, 12:16, :])]
        presum = sb("presum", [P, 2 * HEADS, G], F32)
        den_s = sb("den_s", [P, G], F32)
        den_r = sb("den_r", [P, HEADS * CHH * G // P], F32)
        inv_b = sb("inv_b", [P, PAIRS, CHH, G], F32)
        acc = sb("acc", [P, PAIRS, G], F32)
        ctx_t = sb("ctx_t", [P, PAIRS, G], F32)
        tg = sb("tg", [P, T, F], F32)
        xbg = sb("xbg", [P, T, F], F32)
        x1g = xbg
        h1t = ctx_t[:, :, :].rearrange("p a n -> p (a n)").bitcast(F16).rearrange("p (a k n) -> p a k n", a=2, k=KB)
        s12 = sb("s12", [P, 2, NB], F32)
        lt = sb("lt", [P, 11 * T], F32)
        kept_t = sb("kept_t", [P, 2 * T], F32)
        mx = sb("mx", [P, 2], F32)
        s1t = sb("s1t", [NB, P], F32)
        s2m = sb("s2m", [P, NB], F32)
        b12 = sb("b12", [P, 2, NB], F32)
        hs, hs_r = (x1g[:, :, :].rearrange("p t f -> p (t f)")[:, i * HC:(i + 1) * HC] for i in range(2))
        hs3 = sb("hs3", [P, 3, HC], BF16)
        x1t = inv_b[:, 0, 0:2, :].rearrange("p a (t f) -> p (a t) f", f=F)
        og = inv_b[:, 0, 2:4, :].rearrange("p a (t f) -> p (a t) f", f=F)
        rden = sb("rden", [P, T], F32)
        rvec = probs[:, 2:4, :].rearrange("p a n -> p (a n)")
        prob1 = probs[:, 0:2, :].rearrange("p a (c n) -> p (a c) n", c=CB)
        scaled = presum[:, 0:4, :]

        ps_s = [pb(f"ps_s{i}", [P, CB * G]) for i in range(2)]
        ps_n = [pb(f"ps_n{i}", [P, G]) for i in range(2)]
        ps_d = pb("ps_d", [P, G])
        ps_x = pb("ps_x", [P, G])
        kq_ps = [ps_n[0][:, :], ps_n[1][:, :], ps_s[1][:, 0:G], ps_s[1][:, G:2 * G]]
        acc1 = [ps_s[t // 2][:, G * (t % 2):G * (t % 2) + HC] for t in range(T)]

        const_in = sem("const_in")
        wst_in = [sem(f"wst_in{i}") for i in range(2)]
        wst_used = sem("wst_used")
        adj_in = [sem(f"adj_in{i}") for i in range(2)]
        adj_used = sem("adj_used")
        pool_set = sem("pool_set")
        counted_blocks = sem("counted_blocks")
        mask_bf_ready = sem("mask_bf_ready")
        count_done = sem("count_done")
        setup_done = sem("setup_done")
        step = sem("step")
        x_in = [sem(f"x_in{i}") for i in range(2)]
        var_a = sem("var_a")
        inv_a = sem("inv_a")
        stats_a = sem("stats_a")
        h_ready = sem("h_ready")
        h_turned = sem("h_turned")
        ht_hi = sem("ht_hi")
        ht_ready = sem("ht_ready")
        proj_ready = sem("proj_ready")
        kq_hi = sem("kq_hi")
        kq_ready = sem("kq_ready")
        kq_out = [sem(f"kq_out{i}") for i in range(2)]
        v_ready = sem("v_ready")
        ks_in = sem("ks_in")
        q_in = [sem(f"q_in{i}") for i in range(PAIRS)]
        limit_ready = sem("limit_ready")
        scores_ready = sem("scores_ready")
        exp_ready = sem("exp_ready")
        probs_ready = sem("probs_ready")
        presum_ready = sem("presum_ready")
        num_ready = sem("num_ready")
        den_sum = sem("den_sum")
        num_taken = sem("num_taken")
        den_taken = sem("den_taken")
        den_in = sem("den_in")
        inv_ready = sem("inv_ready")
        inv_out = sem("inv_out")
        inv_in = [sem(f"inv_in{i}") for i in range(PAIRS)]
        divided = sem("divided")
        normed = sem("normed")
        tail_in = sem("tail_in")
        kept_ready = sem("kept_ready")
        tail_h = sem("tail_h")
        residual_ready = sem("residual_ready")
        tail_mm = sem("tail_mm")
        tail_taken = sem("tail_taken")
        var_t = sem("var_t")
        inv_t = sem("inv_t")
        centred = sem("centred")
        x1_ready = sem("x1_ready")
        x1_out = sem("x1_out")
        var_u = sem("var_u")
        inv_u = sem("inv_u")
        stats_u = sem("stats_u")
        h1_ready = sem("h1_ready")
        h1t_hi = sem("h1t_hi")
        s1_turned = sem("s1_turned")
        s1_taken = sem("s1_taken")
        s1_out = sem("s1_out")
        s2_max = sem("s2_max")
        s2_all = sem("s2_all")
        s2m_ready = sem("s2m_ready")
        b12_ready = sem("b12_ready")
        s1_in = [sem(f"s1_in{i}") for i in range(2)]
        s1_cap = sem("s1_cap")
        r_ready = sem("r_ready")
        hs_ready = sem("hs_ready")
        scaled_ready = sem("scaled_ready")
        prob1_ready = sem("prob1_ready")
        prob1_used = sem("prob1_used")
        agg_ready = sem("agg_ready")
        x1_in = sem("x1_in")
        out_ready = sem("out_ready")
        out_done = sem("out_done")

        chain_a, chain_t, chain_u, chain_d, chain_s = (sem(f"chain_{x}") for x in "atuds")
        counted = [
            chain_a, chain_t, chain_u, chain_d, chain_s, *x_in, var_a, inv_a, stats_a, h_ready,
            h_turned, ht_hi, ht_ready, proj_ready, kq_hi, kq_ready, *kq_out, v_ready, ks_in, *q_in, limit_ready,
            scores_ready, exp_ready, probs_ready, presum_ready, num_ready, num_taken, den_sum, den_taken, den_in, inv_ready, inv_out, *inv_in,
            divided, normed, tail_in, kept_ready, tail_h, residual_ready, tail_mm, tail_taken, var_t, inv_t, centred, x1_ready, x1_out, var_u, inv_u,
            stats_u, h1_ready, h1t_hi, s1_turned, s1_taken, s1_out, s2_max, s2_all, s2m_ready, b12_ready, *s1_in, s1_cap, r_ready,
            hs_ready, scaled_ready, prob1_ready, prob1_used, agg_ready, x1_in, out_ready, out_done,
        ]

        block = ctx.enter_context(nc.Block())

        BETWEEN = [
            (w.rstrip("0123456789"), int(w[len(w.rstrip("0123456789")):] or 0)) for w in (
                "norm0 shift1 turn0 high0 norm1 low0 invert make0 make1 turn1 take0 high1 make2 take1 low1 make3 "
                "take2 make4 take3 stats2 take4 make5 residual shift2 norm2 take5 make6 make7 turn2 take6 make8 "
                "take7 high2 take8 make9 divide0 low2 take9 make10 divide1 take10 make11 divide2 make12 take11 make13 "
                "divide3 out0 stats3 add0 out1 shift3 norm3 add1 var take12 turn3 high3 take13 make14 "
                "x_new make15 var_u take14 make16 take15 low3 take16 shift_u make17 rectify turn_h0 take17 make18 "
                "low_h0 turn_h1 take18 low_h1 features0 take_f0 features1 take_f1 s take_s").split()]
        EARLY = [("stats", 0), ("stats", 1), ("shift", 0)]
        PROJECT = EARLY + [x for x in BETWEEN if x[0] in ("stats", "shift", "norm", "turn", "high", "low", "make", "take")]
        LATE = [(w, n) for n in range(sum(w == "make" for w, _ in BETWEEN), NG * PROJ) for w in ("make", "take")]

        R_PARTS = ((0, G), (G, N))

        def place(s):
            c, p = s // PAIRS, s % PAIRS
            return HALF * (c // CHH) + CHH * p + c % CHH

        def halfs_slots(half):
            return [HALF * half + PAIRS * c + p for p in range(PAIRS) for c in range(CHH)]

        DIVIDE_FIRST = dict(zip(range(11, SLOTS), (halfs_slots(0)[i:j] for i, j in ((0, 1), (1, 3), (3, 5), (5, 7), (7, 8)))))
        DIVIDE_SECOND = dict(zip(range(3, 7), (halfs_slots(1)[i:i + 2] for i in range(0, HALF, 2))))

        def hold(eng):
            eng.nop(nofuse=True)

        wst = [nums[:, 8 + i, :].rearrange("p (k f) -> p k f", k=KB) for i in range(2)]
        a1_b = [nums[:, 10, i * F:(i + 1) * F] for i in range(2)]
        adj_st = [inv_b[:, i, :, :].rearrange("p a n -> p (a n)").bitcast(I32) for i in range(2)]
        count, *mask_bf = (presum[:, 2 * i:2 * i + 2, :].rearrange("p a n -> p (a n)").bitcast(BF16) for i in range(3))

        def masks_after(n):
            return range(n * NB // (NG * PROJ), (n + 1) * NB // (NG * PROJ))

        @block.sync
        def _(sp):
            for s in counted:
                sp.sem_inc(s, CREDIT)

            def load_const(dst, src):
                sp.dma_start(dst, src).then_inc(const_in, 16)

            load_const(wo[:, :, :], wo_t.rearrange("(k p) o -> p k o", p=P))
            for i, t in enumerate((bq, bk)):
                with nc.allow_non_contiguous_dma(reason="one small column per partition"):
                    load_const(bias_qk[:, i, :], t.rearrange("(k p) -> p k", p=P))
            for dst, t in ((bv_b, bv), (bo_b, bo), (gamma_b, gamma), (beta_b, beta)):
                load_const(dst[:, :], t.rearrange("(a f) -> a f", a=1).to_broadcast([P, F]))
            for i in range(2):
                load_const(a1_b[i], a1[i:i + 1, :].to_broadcast([P, F]))
            for i, w in enumerate((wq_t, wk_t, wv_t, w1)):
                if i >= 2:
                    sp.wait_ge(wst_used, i - 1)
                sp.dma_start(wst[i % 2], w.rearrange("(k p) o -> p k o", p=P)).then_inc(wst_in[i % 2], 16)

            def load_adj(blocks):
                for c in blocks:
                    if c >= 2:
                        sp.wait_ge(adj_used, c - 1)
                    sp.dma_start(adj_st[c % 2], adj_t[c * P:(c + 1) * P, :]).then_inc(adj_in[c % 2], 16)

            def load_x(b, g, gi):
                if g >= 2:
                    sp.wait_ge(h_ready, gi - 1 + CREDIT)
                sp.dma_start(xg[g % 2], rows(x, b, g)).then_inc(x_in[g % 2], 16)

            def store_projected(b, g, gi):
                sp.wait_ge(kq_ready, 4 * gi + 4 + CREDIT)
                sp.dma_start(kq_d[b, :, :, bass.ds(g * G, G)].rearrange("i (k p) n -> p (i k) n", p=P),
                             kq_s[g][:, :, :, :].rearrange("p i k n -> p (i k) n")).then_inc(kq_out[min(g, 1)], 16)

            def load_q(b, g, pair):
                for half in range(2):
                    for h in (2 * pair, 2 * pair + 1):
                        sp.dma_start(qs[half * DH:(half + 1) * DH, :, h, :],
                                     kq_d[b, 2:4, h * DH:(h + 1) * DH, bass.ds(g * G, G)]
                                     .rearrange("i d n -> d i n")).then_inc(q_in[pair], 16)

            def load_tail(b, g, gi):
                sp.wait_ge(x1_out, 16 * gi + CREDIT)
                hold(sp)
                sp.wait_ge(h1_ready, gi + CREDIT)
                sp.dma_start(xbg[:, :, :], rows(x, b, g)).then_inc(tail_in, 16)

            def store_x1(b, g, gi):
                sp.wait_ge(x1_ready, gi + 1 + CREDIT)
                sp.dma_start(rows(x1_d, b, g), x1g[:, :, :]).then_inc(x1_out, 16)

            def spread(b, g, gi, half):
                hg_i = 2 * gi + half
                sp.wait_ge(den_taken, hg_i + 1 + CREDIT)
                hold(sp)
                sp.wait_ge(inv_ready, hg_i + CREDIT)
                hold(sp)
                sp.wait_ge(inv_out, 16 * hg_i + CREDIT)
                rows_h = P // HEADS
                for h in range(HEADS):
                    sp.dma_start(den_r[rows_h * h:rows_h * (h + 1), :], den_s[32 * h:32 * h + CHH, :]
                                 .rearrange("c (i n) -> c i n", i=rows_h // CHH)).then_inc(den_in, 16)
                sp.wait_ge(inv_ready, hg_i + 1 + CREDIT)
                sp.dma_start(inv_d[b, g, half, :, :], den_r[:, :]).then_inc(inv_out, 16)
                sp.wait_ge(normed, SLOTS * gi + HALF * half + CREDIT)
                hold(sp)
                sp.wait_ge(inv_out, 16 * (hg_i + 1) + CREDIT)
                for h in range(HEADS):
                    sp.dma_start(inv_b[h % 2 * DH:(h % 2 + 1) * DH, h // 2, :, :],
                                 inv_d[b, g, half, rows_h * h:rows_h * (h + 1), :]
                                 .rearrange("r n -> (r n)").rearrange("(a c n) -> a c n", a=1, c=CHH)
                                 .to_broadcast([DH, CHH, G])).then_inc(inv_in[h // 2], 16)

            def store_out(b, g, gi):
                sp.wait_ge(out_ready, 4 * gi + 4 + CREDIT)
                sp.dma_start(rows(out, b, g), og[:, :, :]).then_inc(out_done, 16)

            def finish_projection(b, n, g0):
                store_projected(b, NG - 1, g0 + NG - 1)
                sp.wait_ge(kq_out[0], 16 * n + CREDIT)
                hold(sp)
                sp.wait_ge(kq_out[1], 16 * (NG - 1) * n + CREDIT)
                hold(sp)
                for part in range(2):
                    sp.dma_start(ks[part * DH:(part + 1) * DH, :, :],
                                 kq_d[b, part, :, :].rearrange("(h d) n -> d h n", d=DH)).then_inc(ks_in, 16)
                for pair in range(PAIRS):
                    load_q(b, 0, pair)

            load_x(0, 0, 0)
            load_x(0, 1, 1)
            load_adj(range(0, 3))
            load_x(0, 2, 2)
            load_adj(range(3, 6))
            store_projected(0, 0, 0)
            load_x(0, 3, 3)
            load_adj(range(6, 9))
            store_projected(0, 1, 1)
            load_adj(range(9, 13))
            store_projected(0, 2, 2)
            load_adj(range(13, NB))
            finish_projection(0, 1, 0)

            with sp.Fori(0, B) as b:
                sp.wait_ge(out_done, 16 * NG * b + CREDIT)
                hold(sp)
                spread(b, 0, NG * b, 0)

                with sp.Fori(1, NG) as g:
                    gi = NG * b + g
                    for pair in range(PAIRS):
                        sp.wait_ge(scores_ready, UNITS * gi - 2 * (PAIRS - 1 - pair) + CREDIT)
                        load_q(b, g, pair)
                    load_tail(b, g - 1, gi - 1)
                    spread(b, g - 1, gi - 1, 1)
                    spread(b, g, gi, 0)
                    store_x1(b, g - 1, gi - 1)
                gl = NG * b + NG - 1
                g0 = NG * b + NG
                nb = (b + 1) % B
                load_tail(b, NG - 1, gl)
                sp.wait_ge(normed, SLOTS * gl + CHH + CREDIT)
                hold(sp)
                load_x(nb, 0, g0)
                load_x(nb, 1, g0 + 1)
                spread(b, NG - 1, gl, 1)
                load_x(nb, 2, g0 + 2)
                store_projected(b + 1, 0, g0)
                load_x(nb, 3, g0 + 3)
                store_projected(b + 1, 1, g0 + 1)
                store_x1(b, NG - 1, gl)
                store_projected(b + 1, 2, g0 + 2)

                sp.wait_ge(s1_taken, b + 1 + CREDIT)
                sp.dma_start(s1_d[b, :, :], s1t[:, :]).then_inc(s1_out, 16)
                sp.wait_ge(s1_out, 16 * (b + 1) + CREDIT)
                sp.wait_ge(x1_out, 16 * (NG * b + NG) + CREDIT)
                hold(sp)
                for i, (at, to) in enumerate(R_PARTS):
                    sp.dma_start(rvec[:, at:to], s1_d[b, at // P:to // P, :].rearrange("m p -> (m p)")
                                 .rearrange("(a n) -> a n", a=1).to_broadcast([P, to - at])).then_inc(s1_in[i], 16)
                finish_projection(b + 1, b + 2, g0)
                with sp.Fori(0, NG) as g:
                    gi = NG * b + g
                    sp.wait_ge(out_ready, 4 * gi + CREDIT)
                    sp.dma_start(x1t[:, :, :], rows(x1_d, b, g)).then_inc(x1_in, 16)
                    store_out(b, g, gi)
            sp.wait_ge(out_done, 16 * NG * B + CREDIT)

        def work_views(work):
            return (work[:, 0:6 * T].rearrange("p (t s) -> p t s", t=T), work[:, 6 * T:8 * T].rearrange("p (t s) -> p t s", t=T),
                    work[:, 8 * T:9 * T], work[:, 9 * T:10 * T], work[:, 10 * T:11 * T])

        def variances(dve, src, work, done, chain, n):
            st, mv, var, _, _ = work_views(work)
            for t in range(T):
                last = nc.vector.bn_stats(st[:, t, :], src[:, t, :])
            last.then_inc(chain, 1)
            dve.wait_ge(chain, n + 1 + CREDIT)
            hold(dve)
            for t in range(T):
                last = nc.vector.bn_aggr(mv[:, t, :], st[:, t:t + 1, :])
            last.then_inc(chain, 1)
            dve.wait_ge(chain, n + 2 + CREDIT)
            nc.vector.tensor_scalar(var, mv[:, :, 1], EPS, None, ALU.add).then_inc(done, 1)

        def inverse_deviations(work, inv, done):
            var = work_views(work)[2]
            nc.gpsimd.tensor_tensor(inv, var, minus_half[:, :], ALU.pow).then_inc(done, 1)

        def shifts(work, inv, shift, done):
            mv = work_views(work)[1]
            nc.vector.scalar_tensor_tensor(out=shift, in0=mv[:, :, 0], scalar=-1.0, in1=inv,
                                           op0=ALU.mult, op1=ALU.mult).then_inc(done, 1)

        def norm_args(inv, shift, t):
            return dict(scale=inv[:, t:t + 1], bias=shift[:, t:t + 1])

        @block.gpsimd
        def _(pool):
            nc.gpsimd.memset(ident[:, :], 0.0).then_inc(pool_set, 1)
            pool.wait_ge(pool_set, 1)
            nc.gpsimd.affine_select(out=ident[:, :], in_=ident[:, :], compare_op=ALU.not_equal, fill=1.0,
                                    base=0, pattern=[[-1, P]], channel_multiplier=1).then_inc(pool_set, 1)
            nc.gpsimd.memset(minus_half[:, :], -0.5)
            nc.gpsimd.memset(h2[:, :, F:HC], 1.0).then_inc(pool_set, 1)
            nc.gpsimd.memset(count, 0.0).then_inc(counted_blocks, 1)
            pool.wait_ge(const_in, 16 * 9)

            def deviations_a(gi, g):
                pool.wait_ge(var_a, gi + 1 + CREDIT)
                pool.wait_ge(pool_set, 3)
                pool.wait_ge(kept_ready, gi - NG + 1 + CREDIT)
                inverse_deviations(ln[g % 2], kept[:, g, 0:T], inv_a)

            def tail_step(gi, s):
                if s in (RESIDUAL, RESIDUAL + 1):
                    pool.wait_ge(tail_h, 2 * gi + 2 + CREDIT)
                    dst, c = (tg, bo_b) if s == RESIDUAL else (xbg, beta_b)
                    for t in range(T):
                        last = nc.gpsimd.tensor_tensor(dst[:, t, :], dst[:, t, :], c[:, :], ALU.add)
                    last.then_inc(residual_ready, 1)
                if s == VAR_T:
                    pool.wait_ge(var_t, gi + 1 + CREDIT)
                    inverse_deviations(lt, work_views(lt)[3], inv_t)
                if s == VAR_U:
                    pool.wait_ge(var_u, gi + 1 + CREDIT)
                    inverse_deviations(lt, work_views(lt)[3], inv_u)

            RESIDUAL, VAR_T, VAR_U = 5, 9, 11

            def attend(gi, g, tail):
                for s in range(SLOTS):
                    if tail:
                        tail_step(gi - 1, s)
                    for u in (2 * s, 2 * s + 1):
                        pool.wait_ge(probs_ready, UNITS * gi + u + 1 + CREDIT)
                        pool.wait_ge(den_sum, CH * gi + s // PAIRS - 1 + CREDIT)
                        nc.gpsimd.tensor_tensor(presum[:, u % (2 * HEADS), :], probs[:, u % 4, 0:G],
                                                probs[:, u % 4, G:2 * G], ALU.add).then_inc(presum_ready, 1)

            for task, n in PROJECT + LATE:
                if task == "stats":
                    deviations_a(n, n)
                if task == "take":
                    for c in masks_after(n):
                        pool.wait_ge(mask_bf_ready, c + 1)
                        pool.wait_ge(counted_blocks, c + 1)
                        nc.gpsimd.tensor_tensor(count, count, mask_bf[c % 2], ALU.add).then_inc(counted_blocks, 1)
            with pool.Fori(0, B) as b:
                attend(NG * b, 0, False)
                with pool.Fori(1, NG) as g:
                    attend(NG * b + g, g, True)
                for n in range(2):
                    deviations_a(NG * b + NG + n, n)
                for task, n in BETWEEN:
                    if task == "stats":
                        deviations_a(NG * b + NG + n, n)
                    if task == "residual":
                        tail_step(NG * b + NG - 1, RESIDUAL)
                        tail_step(NG * b + NG - 1, RESIDUAL + 1)
                    if task == "var":
                        tail_step(NG * b + NG - 1, VAR_T)
                    if task == "var_u":
                        tail_step(NG * b + NG - 1, VAR_U)
                pool.wait_ge(s2_max, b + 1 + CREDIT)
                hold(pool)
                nc.gpsimd.partition_all_reduce(mx[:, 1:2], mx[:, 0:1], P, RMAX).then_inc(s2_all, 1)

        @block.vector
        def _(dve):
            steps = [0]
            cur_b = [0]

            def link(ins):
                steps[0] += 1
                ins.then_inc(step, 1)
                dve.wait_ge(step, steps[0])

            link(nc.vector.memset(pick[:, :], 0.0))
            link(nc.vector.memset(pick[:, CHH - 1::CHH], 1.0))
            nc.vector.memset(exp_lo[:, :], EXP_LO)
            link(nc.vector.memset(ones_bf[:, :], 1.0))
            dve.wait_ge(const_in, 16 * 9)
            for i in range(4):
                dve.wait_ge(wst_in[i % 2], 16 * (i // 2 + 1))
                if i < 3:
                    dst, src = wqkv[i], wst[i % 2]
                else:
                    ext = tg[:, 0:3, :].rearrange("p t f -> p (t f)")[:, 0:KB * W1C].rearrange("p (k c) -> p k c", k=KB)
                    prod = x1g[:, 0:2 * KB, :]
                    for k in range(KB):
                        nc.vector.tensor_copy(ext[:, k, 0:F], wst[1][:, k, :])
                        for j in range(2):
                            last = nc.vector.tensor_tensor(prod[:, 2 * k + j, :], wst[1][:, k, :], a1_b[j], ALU.mult)
                    link(last)
                    for k in range(KB):
                        last = nc.vector.tensor_reduce(ext[:, k, F:F + 2], prod[:, 2 * k:2 * k + 2, :], AX_X, ALU.add)
                    link(last)
                    dst, src = w1s, ext
                link(nc.vector.tensor_copy(dst[:, 0, :, :], src))
                steps[0] += 1
                nc.vector.tensor_tensor(dst[:, 1, :, :], src, dst[:, 0, :, :], ALU.subtract).then_inc(step, 1)
                dve.wait_ge(step, steps[0])
                dve.sem_inc(wst_used, 1)
            def stats(gi, g, xi):
                dve.wait_ge(x_in[g % 2], 16 * xi + CREDIT)
                dve.wait_ge(inv_a, gi - 1 + CREDIT)
                dve.wait_ge(stats_a, gi - 1 + CREDIT)
                variances(dve, xg[g % 2], ln[g % 2], var_a, chain_a, 2 * gi)

            def shift(gi, g):
                dve.wait_ge(inv_a, gi + 1 + CREDIT)
                shifts(ln[g % 2], kept[:, g, 0:T], kept[:, g, T:2 * T], stats_a)

            def low(gi, g):
                dve.wait_ge(ht_hi, gi + 1 + CREDIT)
                nc.vector.tensor_tensor(ht[g % 2][:, 1, :], ps_s[0][:, :], ht[g % 2][:, 0, :], ALU.subtract)\
                    .then_inc(ht_ready, 1)

            def project(gi, g, i):
                if i < 4:
                    dve.wait_ge(kq_hi, 4 * gi + i + 1 + CREDIT)
                    w, k = 1 - i // 2, i % 2
                    nc.vector.scalar_tensor_tensor(
                        out=kq_s[g][:, 2 * (i // 2) + 1, k, :], in0=kq_ps[i], scalar=bias_qk[:, w, k:k + 1],
                        in1=kq_s[g][:, 2 * (i // 2), k, :], op0=ALU.add, op1=ALU.subtract).then_inc(kq_ready, 1)
                    return
                dve.wait_ge(proj_ready, PROJ * gi + i + 1 + CREDIT)
                for t in range(2):
                    last = nc.vector.tensor_tensor(v[:, T * g + 2 * (i - 4) + t, :], ps_d[:, t * F:(t + 1) * F],
                                                   bv_b[:, :], ALU.add)
                last.then_inc(v_ready, 1)

            def bound(gi, u):
                dve.wait_ge(exp_ready, UNITS * gi + u + 1 + CREDIT)
                if u % HEADS == 0:
                    dve.wait_ge(limit_ready, CH * gi + u // HEADS + 1 + CREDIT)
                dve.wait_ge(presum_ready, UNITS * gi + u - 3 + CREDIT)
                dve.wait_ge(num_ready, SLOTS * gi + u // 2 - 1 + CREDIT)
                nc.vector.scalar_tensor_tensor(
                    out=probs[:, u % 4, :], in0=ps_s[u % 2][:, :], scalar=EXP_LO,
                    in1=limit[u // HEADS % 3][:, :, :].rearrange("p c n -> p (c n)"),
                    op0=ALU.max, op1=ALU.min).then_inc(probs_ready, 1)

            def invert(gi, half):
                dve.wait_ge(den_in, 64 * (2 * gi + half + 1) + CREDIT)
                nc.vector.reciprocal(den_r[:, :], den_r[:, :]).then_inc(inv_ready, 1)

            def divide(gi, slots):
                for s in slots:
                    c, p = s // PAIRS, s % PAIRS
                    dve.wait_ge(inv_in[p], 32 * (2 * gi + c // CHH + 1) + CREDIT)
                    dve.wait_ge(num_taken, SLOTS * gi + s + 1 + CREDIT)
                    dst = acc[:, p, :] if c == 0 else nums[:, place(s), :]
                    nc.vector.tensor_tensor(dst, nums[:, place(s), :], inv_b[:, p, c % CHH, :], ALU.mult)\
                        .then_inc(divided, 1)
                for s in slots:
                    c, p = s // PAIRS, s % PAIRS
                    n = place(s)
                    dve.wait_ge(divided, SLOTS * gi + n + 1 + CREDIT)
                    dve.wait_ge(normed, SLOTS * gi + n + CREDIT)
                    if c == 0:
                        dve.sem_inc(normed, 1)
                        continue
                    dst = ctx_t if c == CH - 1 else acc
                    if c == CH - 1:
                        dve.wait_ge(tail_mm, TURNS * gi + CREDIT)
                    nc.vector.tensor_tensor(dst[:, p, :], acc[:, p, :], nums[:, place(s), :], ALU.add).then_inc(normed, 1)

            def tail_add(gi, a):
                if a == 0:
                    dve.wait_ge(residual_ready, 2 * gi + 1 + CREDIT)
                dve.wait_ge(tail_mm, TURNS * gi + a + 1 + CREDIT)
                nc.vector.tensor_tensor(tg[:, 2 * a:2 * a + 2, :],
                                        ps_x[:, :].rearrange("p (t f) -> p t f", t=2),
                                        tg[:, 2 * a:2 * a + 2, :], ALU.add).then_inc(tail_taken, 1)

            def tail_var(gi):
                dve.wait_ge(tail_taken, TURNS * gi + 2 + CREDIT)
                variances(dve, tg, lt, var_t, chain_t, 2 * gi)

            def tail_x1(gi):
                dve.wait_ge(inv_t, gi + 1 + CREDIT)
                dve.wait_ge(residual_ready, 2 * gi + 2 + CREDIT)
                _, mv, _, inv, _ = work_views(lt)
                for t in range(T):
                    last = nc.vector.scalar_tensor_tensor(out=tg[:, t, :], in0=tg[:, t, :], scalar=mv[:, t, 0:1],
                                                          in1=gamma_b[:, :], op0=ALU.subtract, op1=ALU.mult)
                last.then_inc(centred, 1)
                dve.wait_ge(centred, gi + 1 + CREDIT)
                for t in range(T):
                    last = nc.vector.scalar_tensor_tensor(out=x1g[:, t, :], in0=tg[:, t, :], scalar=inv[:, t:t + 1],
                                                          in1=xbg[:, t, :], op0=ALU.mult, op1=ALU.add)
                last.then_inc(x1_ready, 1)

            def tail_var_u(gi):
                dve.wait_ge(x1_ready, gi + 1 + CREDIT)
                variances(dve, x1g, lt, var_u, chain_u, 2 * gi)

            def tail_shift(gi):
                dve.wait_ge(inv_u, gi + 1 + CREDIT)
                shifts(lt, *work_views(lt)[3:5], stats_u)

            def tail_low(gi, k):
                dve.wait_ge(h1t_hi, KB * gi + k + 1 + CREDIT)
                nc.vector.tensor_tensor(h1t[:, 1, k, :], ps_x[:, :], h1t[:, 0, k, :], ALU.subtract)\
                    .then_inc(tail_taken, 1)

            def attend(gi, start, prev, more):
                if start:
                    bound(gi, 0)
                    bound(gi, 1)
                for s in range(SLOTS):
                    if prev:
                        finish_early(gi - 1, s)
                    if s + 1 < SLOTS:
                        bound(gi, 2 * s + 2)
                        bound(gi, 2 * s + 3)
                    elif more:
                        bound(gi + 1, 0)
                        bound(gi + 1, 1)
                    if prev:
                        finish_step(gi - 1, s)
                    if s == HALF + 1:
                        invert(gi, 0)
                    divide(gi, DIVIDE_FIRST.get(s, ()))
                    if not more:
                        for task, n in {SLOTS - 2: EARLY[0:1], SLOTS - 1: EARLY[1:3]}.get(s, ()):
                            task_a(gi + 1, cur_b[0] + 1, task, n)

            def finish_early(gi, s):
                if s in (13, 14):
                    tail_low(gi, s - 13)

            def finish_step(gi, s):
                if s == 1:
                    invert(gi, 1)
                divide(gi, DIVIDE_SECOND.get(s, ()))
                if s == 7:
                    tail_add(gi, 0)
                if s == 8:
                    tail_add(gi, 1)
                    tail_var(gi)
                if s == 9:
                    tail_x1(gi)
                if s == 10:
                    tail_var_u(gi)
                if s == 11:
                    tail_shift(gi)

            def aggregate(gi, mb):
                dve.wait_ge(scaled_ready, NB * gi + mb + 1 + CREDIT)
                if mb == 3:
                    dve.wait_ge(agg_ready, T * gi + CREDIT)
                else:
                    dve.wait_ge(prob1_used, (NB - 1) * gi + (mb - 2 if mb < 3 else mb - 3) + CREDIT)
                nc.vector.scalar_tensor_tensor(
                    out=prob1[:, mb % 4, :], in0=scaled[:, mb % 4, :], scalar=b12[:, 1, mb:mb + 1],
                    in1=mask[:, mb, bass.ds(self_g[0] * G, G)], op0=ALU.max, op1=ALU.mult).then_inc(prob1_ready, 1)

            self_g = [0]

            def emit(gi):
                dve.wait_ge(x1_in, 16 * (gi + 1) + CREDIT)
                dve.wait_ge(out_done, 16 * gi + CREDIT)
                for t in range(T):
                    dve.wait_ge(agg_ready, T * gi + t + 1 + CREDIT)
                    dve.wait_ge(out_ready, T * gi + t + CREDIT)
                    nc.vector.reciprocal(rden[:, t:t + 1], acc1[t][:, F:HC]).then_inc(chain_d, 1)
                    dve.wait_ge(chain_d, T * gi + t + 1 + CREDIT)
                    nc.vector.scalar_tensor_tensor(out=og[:, t, :], in0=acc1[t][:, 0:F], scalar=rden[:, t:t + 1],
                                                   in1=x1t[:, t, :], op0=ALU.mult, op1=ALU.add).then_inc(out_ready, 1)

            S_LINKS = 5
            def task_a(g0, b, task, n):
                if task == "stats":
                    stats(g0 + n, n, NG // 2 * b + n // 2 + 1)
                if task == "shift":
                    shift(g0 + n, n)
                if task == "low":
                    low(g0 + n, n)
                if task == "take":
                    project(g0 + n // PROJ, n // PROJ, n % PROJ)

            for task, n in PROJECT + LATE:
                task_a(0, 0, task, n)
                if task == "take":
                    for c in masks_after(n):
                        dve.wait_ge(adj_in[c % 2], 16 * (c // 2 + 1))
                        nc.vector.tensor_scalar(mask[:, c, :], adj_st[c % 2], 0, None, ALU.not_equal).then_inc(adj_used, 1)
            dve.wait_ge(count_done, 1)
            for i in range(2):
                nc.vector.tensor_scalar(no_nb[:, i * CB * G:(i + 1) * CB * G], ps_s[i][:, :], 0.5, None, ALU.is_lt)\
                    .then_inc(setup_done, 1)
            with dve.Fori(0, B) as b:
                cur_b[0] = b
                attend(NG * b, True, False, True)
                with dve.Fori(1, NG - 1) as g:
                    attend(NG * b + g, False, True, True)
                gl = NG * b + NG - 1
                attend(gl, False, True, False)
                for task, n in BETWEEN:
                    task_a(gl + 1, b + 1, task, n)
                    if task == "invert":
                        invert(gl, 1)
                    if task == "divide":
                        divide(gl, halfs_slots(1)[2 * n:2 * n + 2])
                    if task == "add":
                        tail_add(gl, n)
                    if task == "var":
                        tail_var(gl)
                    if task == "x_new":
                        tail_x1(gl)
                    if task == "var_u":
                        tail_var_u(gl)
                    if task == "shift_u":
                        tail_shift(gl)
                    if task == "low_h":
                        tail_low(gl, n)

                dve.wait_ge(tail_taken, TURNS * (gl + 1) + CREDIT)
                nc.vector.tensor_reduce(mx[:, 0:1], s12[:, 1, :], AX_X, ALU.max).then_inc(s2_max, 1)
                dve.wait_ge(s1_turned, b + 1 + CREDIT)
                dve.wait_ge(s1_out, 16 * b + CREDIT)
                nc.vector.tensor_copy(s1t[:, :], ps_x[0:NB, 0:P]).then_inc(s1_taken, 1)
                for task, n in LATE:
                    task_a(gl + 1, b + 1, task, n)
                dve.wait_ge(s2_all, b + 1 + CREDIT)
                nc.vector.tensor_scalar(s2m[:, :], s12[:, 1, :], mx[:, 1:2], None, ALU.subtract).then_inc(s2m_ready, 1)
                for i, (at, to) in enumerate(R_PARTS):
                    dve.wait_ge(s1_in[i], 16 * (b + 1) + CREDIT)
                    nc.vector.tensor_scalar(rvec[:, at:to], rvec[:, at:to], mx[:, 1:2], R_CAP, ALU.add, ALU.min)\
                        .then_inc(s1_cap, 1)
                n = [0]

                def link_b(ins):
                    n[0] += 1
                    ins.then_inc(chain_s, 1)
                    dve.wait_ge(chain_s, S_LINKS * b + n[0] + CREDIT)

                def sum_features():
                    dve.wait_ge(x1_out, 16 * NG * (b + 1) + CREDIT)
                    link_b(nc.vector.tensor_reduce(hs[:, :], h2[:, :, :].rearrange("p m f -> p f m"), AX_X, ALU.add))
                    link_b(nc.vector.tensor_copy(hs3[:, 0, :], hs[:, :]))
                    link_b(nc.vector.tensor_tensor(hs_r[:, :], hs[:, :], hs3[:, 0, :], ALU.subtract))
                    link_b(nc.vector.tensor_copy(hs3[:, 1, :], hs_r[:, :]))
                    link_b(nc.vector.tensor_tensor(hs[:, :], hs_r[:, :], hs3[:, 1, :], ALU.subtract))
                    nc.vector.tensor_copy(hs3[:, 2, :], hs[:, :]).then_inc(hs_ready, 1)

                dve.wait_ge(b12_ready, 2 * b + 2 + CREDIT)

                self_g[0] = 0
                for mb in range(NB):
                    aggregate(NG * b, mb)
                    if mb == NB // 4:
                        sum_features()
                with dve.Fori(1, NG) as g:
                    self_g[0] = g
                    for mb in range(NB):
                        aggregate(NG * b + g, mb)
                        if mb == 2:
                            emit(NG * b + g - 1)
                emit(gl)

        @block.scalar
        def _(act):
            def norm(gi, g):
                act.wait_ge(stats_a, gi + 1 + CREDIT)
                act.wait_ge(h_turned, gi + CREDIT)
                for t in range(T):
                    last = nc.scalar.activation(hg[:, t, :], xg[g % 2][:, t, :], ACT.Relu,
                                                **norm_args(kept[:, g, 0:T], kept[:, g, T:2 * T], t))
                last.then_inc(h_ready, 1)

            def high(gi, g):
                act.wait_ge(h_turned, gi + 1 + CREDIT)
                act.wait_ge(proj_ready, PROJ * (gi - 1) + CREDIT)
                nc.scalar.copy(ht[g % 2][:, 0, :], ps_s[0][:, :]).then_inc(ht_hi, 1)

            def project(gi, g, i, n):
                if i >= 4:
                    return
                act.wait_ge(proj_ready, PROJ * gi + i + 1 + CREDIT)
                if g == 2 and i == 0:
                    act.wait_ge(kq_out[0], 16 * n + CREDIT)
                w, k = 1 - i // 2, i % 2
                nc.scalar.activation(kq_s[g][:, 2 * (i // 2), k, :], kq_ps[i], ACT.Identity,
                                     bias=bias_qk[:, w, k:k + 1]).then_inc(kq_hi, 1)


            def exp(gi, u):
                act.wait_ge(scores_ready, UNITS * gi + u + 1 + CREDIT)
                nc.scalar.activation(ps_s[u % 2][:, :], ps_s[u % 2][:, :], ACT.Exp, scale=DH ** -0.5).then_inc(exp_ready, 1)

            def take_num(gi, s):
                act.wait_ge(num_ready, SLOTS * gi + s + 1 + CREDIT)
                act.wait_ge(normed, SLOTS * gi - (HALF if s < HALF else 0) + CREDIT)
                nc.scalar.copy(nums[:, place(s), :], ps_n[s % 2][:, :]).then_inc(num_taken, 1)

            def take_den(gi, half):
                act.wait_ge(den_sum, CH * gi + CHH * (half + 1) + CREDIT)
                act.wait_ge(den_in, 64 * (2 * gi + half) + CREDIT)
                nc.scalar.copy(den_s[:, :], ps_d[:, :]).then_inc(den_taken, 1)

            def take_kept(gi, g):
                act.wait_ge(tail_h, 2 * gi + CREDIT)
                hold(act)
                nc.scalar.copy(kept_t[:, :].unsqueeze(1), kept[:, bass.ds(g, 1), :]).then_inc(kept_ready, 1)

            def renew_h(gi, half):
                if half == 0:
                    act.wait_ge(tail_in, 16 * (gi + 1) + CREDIT)
                    act.wait_ge(kept_ready, gi + 1 + CREDIT)
                    act.wait_ge(tail_mm, TURNS * (gi - 1) + 4 + CREDIT)
                for t in (2 * half, 2 * half + 1):
                    last = nc.scalar.activation(tg[:, t, :], xbg[:, t, :], ACT.Relu,
                                                **norm_args(kept_t[:, 0:T], kept_t[:, T:2 * T], t))
                last.then_inc(tail_h, 1)

            def rectify(gi):
                act.wait_ge(stats_u, gi + 1 + CREDIT)
                for t in range(T):
                    last = nc.scalar.activation(tg[:, t, :], x1g[:, t, :], ACT.Relu,
                                                **norm_args(*work_views(lt)[3:5], t))
                last.then_inc(h1_ready, 1)

            def tail_high(gi, k):
                act.wait_ge(tail_mm, TURNS * gi + 3 + k + CREDIT)
                nc.scalar.copy(h1t[:, 0, k, :], ps_x[:, :]).then_inc(h1t_hi, 1)

            def take_features(gi, g, a):
                act.wait_ge(tail_mm, TURNS * gi + 5 + a + CREDIT)
                hold(act)
                nc.scalar.copy(h2[:, bass.ds(T * g + 2 * a, 2), 0:F], ps_x[:, :].rearrange("p (t f) -> p t f", t=2))\
                    .then_inc(tail_taken, 1)

            def take_s(gi, g):
                act.wait_ge(tail_mm, TURNS * gi + 7 + CREDIT)
                hold(act)
                nc.scalar.copy(s12[:, :, bass.ds(T * g, T)], ps_x[:, 0:2 * T].rearrange("p (t c) -> p c t", c=2))\
                    .then_inc(tail_taken, 1)

            def tail_early(gi, g, s):
                if s == 15:
                    take_features(gi, g, 1)

            def tail_step(gi, g, s):
                if s == 2:
                    take_kept(gi, g)
                if s in (3, 4):
                    renew_h(gi, s - 3)
                if s == 11:
                    rectify(gi)
                if s in (12, 13):
                    tail_high(gi, s - 12)
                if s == 14:
                    take_features(gi, g, 0)
                if s == 15:
                    take_s(gi, g)

            def expand(gi, g, c):
                act.wait_ge(probs_ready, UNITS * gi + (HEADS * (c - 2) if c >= 3 else (-HEADS, 0, -2 * HEADS)[c]) + CREDIT)
                hold(act)
                nc.scalar.activation(limit[c % 3][:, :, :], mask[:, CB * c:CB * c + CB, bass.ds(g * G, G)],
                                     ACT.Identity, scale=EXP_HI - EXP_LO, bias=exp_lo[:, :]).then_inc(limit_ready, 1)

            def attend(gi, g, start, prev, more):
                if start:
                    expand(gi, g, 0)
                    expand(gi, g, 1)
                    exp(gi, 0)
                    exp(gi, 1)
                for s in range(SLOTS):
                    if s + 1 < SLOTS:
                        exp(gi, 2 * s + 2)
                        exp(gi, 2 * s + 3)
                    elif more:
                        exp(gi + 1, 0)
                        exp(gi + 1, 1)
                    if prev:
                        tail_early(gi - 1, g - 1, s)
                    take_num(gi, s)
                    if s == HALF:
                        take_den(gi, 0)
                    if s == 0 and prev:
                        take_den(gi - 1, 1)
                    c = s // 2 + 2
                    if s % 2 == 1 and c < CH:
                        expand(gi, g, c)
                    elif s % 2 == 1 and more:
                        expand(gi + 1, g + 1, c - CH)
                    if prev:
                        tail_step(gi - 1, g - 1, s)

            def scale(gi, g, mb):
                act.wait_ge(prob1_ready, NB * gi + max(mb - 3, 0) + CREDIT)
                hold(act)
                nc.scalar.activation(scaled[:, mb % 4, :], rvec[:, bass.ds(g * G, G)], ACT.Copy,
                                     scale=b12[:, 0, mb:mb + 1]).then_inc(scaled_ready, 1)

            def task_a(g0, b, task, n):
                if task == "norm":
                    norm(g0 + n, n)
                if task == "high":
                    high(g0 + n, n)
                if task == "take":
                    project(g0 + n // PROJ, n // PROJ, n % PROJ, b + 1)

            act.wait_ge(const_in, 16 * 9)
            act.wait_ge(wst_used, 4)
            for task, n in PROJECT + LATE:
                task_a(0, 0, task, n)
                if task == "take":
                    for c in masks_after(n):
                        act.wait_ge(adj_used, c + 1)
                        if c >= 2:
                            act.wait_ge(counted_blocks, c)
                        nc.scalar.copy(mask_bf[c % 2], mask[:, c, :]).then_inc(mask_bf_ready, 1)
            act.wait_ge(setup_done, 2)
            with act.Fori(0, B) as b:
                act.wait_ge(kq_out[0], 16 * (b + 1) + CREDIT)
                act.wait_ge(kq_out[1], 16 * (NG - 1) * (b + 1) + CREDIT)
                hold(act)
                attend(NG * b, 0, True, False, True)
                with act.Fori(1, NG - 1) as g:
                    attend(NG * b + g, g, False, True, True)
                gl = NG * b + NG - 1
                attend(gl, NG - 1, False, True, False)
                take_den(gl, 1)
                for task, n in BETWEEN:
                    task_a(gl + 1, b + 1, task, n)
                    if task == "residual":
                        take_kept(gl, NG - 1)
                        renew_h(gl, 0)
                        renew_h(gl, 1)
                    if task == "rectify":
                        rectify(gl)
                    if task == "turn_h":
                        tail_high(gl, n)
                    if task == "take_f":
                        take_features(gl, NG - 1, n)
                    if task == "take_s":
                        take_s(gl, NG - 1)
                for task, n in LATE:
                    task_a(gl + 1, b + 1, task, n)
                act.wait_ge(s2m_ready, b + 1 + CREDIT)
                nc.scalar.activation(b12[:, 0, :], s2m[:, :], ACT.Exp).then_inc(b12_ready, 1)
                nc.scalar.activation(b12[:, 1, :], s2m[:, :], ACT.Exp, scale=SLOPE).then_inc(b12_ready, 1)
                for i, (at, to) in enumerate(R_PARTS):
                    act.wait_ge(s1_cap, 2 * b + i + 1 + CREDIT)
                    nc.scalar.activation(rvec[:, at:to], rvec[:, at:to], ACT.Exp, scale=1.0 - SLOPE).then_inc(r_ready, 1)
                act.wait_ge(b12_ready, 2 * b + 2 + CREDIT)
                act.wait_ge(r_ready, 2 * b + 2 + CREDIT)
                with act.Fori(0, NG) as g:
                    for mb in range(NB):
                        scale(NG * b + g, g, mb)

        @block.tensor
        def _(pe):
            PARTS = ((0, 0), (0, 1), (1, 0))

            pe.wait_ge(pool_set, 3)
            pe.wait_ge(wst_used, 4)

            def turn(gi, g):
                pe.wait_ge(h_ready, gi + 1 + CREDIT)
                pe.wait_ge(ht_ready, gi + CREDIT)
                if g == 0:
                    pe.wait_ge(probs_ready, UNITS * gi + CREDIT)
                for k in range(KB):
                    for t in range(T):
                        mm = nc.tensor.transpose(ps_s[0][:, k * G + t * P:k * G + (t + 1) * P],
                                                 hg[:, t, k * P:(k + 1) * P], ident[:, :])
                mm.then_inc(h_turned, 1)

            def project(gi, g, i):
                h = ht[g % 2]
                if i == 0:
                    pe.wait_ge(ht_ready, gi + 1 + CREDIT)
                    if g == 0:
                        pe.wait_ge(num_taken, SLOTS * gi + CREDIT)
                if i < 4:
                    pe.wait_ge(kq_ready, 4 * gi + i - 3 + CREDIT)
                    w, fb = wqkv[1 - i // 2], i % 2
                    n = 0
                    for k in range(KB):
                        for a, c in PARTS:
                            mm = nc.tensor.matmul(kq_ps[i], w[:, a, k, fb * P:(fb + 1) * P], h[:, c, k * G:(k + 1) * G],
                                                  start=(n == 0), stop=(n == 3 * KB - 1))
                            n += 1
                    mm.then_inc(proj_ready, 1)
                    return
                if g == 0 and i == 4:
                    pe.wait_ge(den_taken, 2 * gi + CREDIT)
                pe.wait_ge(v_ready, 2 * gi + i - 4 + CREDIT)
                for t in range(2):
                    n = 0
                    for k in range(KB):
                        for a, c in PARTS:
                            at = k * G + (2 * (i - 4) + t) * P
                            mm = nc.tensor.matmul(ps_d[:, t * F:(t + 1) * F], h[:, a, at:at + P], wqkv[2][:, c, k, :],
                                                  start=(n == 0), stop=(n == 3 * KB - 1))
                            n += 1
                mm.then_inc(proj_ready, 1)

            def task_a(g0, task, n):
                if task == "turn":
                    turn(g0 + n, n)
                if task == "make":
                    project(g0 + n // PROJ, n // PROJ, n % PROJ)

            def score(gi, u):
                h, c = u % HEADS, u // HEADS
                if c == 0 and h % 2 == 0:
                    pe.wait_ge(q_in[h // 2], 64 * (gi + 1) + CREDIT)
                pe.wait_ge(probs_ready, UNITS * gi + u - 1 + CREDIT)
                for cb in range(CB):
                    for part in range(2):
                        mm = nc.tensor.matmul(ps_s[u % 2][:, cb * G:(cb + 1) * G],
                                              ks[:, h, (CB * c + cb) * P:(CB * c + cb + 1) * P],
                                              qs[:, part, h, :], start=(part == 0), stop=(part == 1))
                mm.then_inc(scores_ready, 1)

            def context(gi, s):
                c, p = s // PAIRS, s % PAIRS
                pe.wait_ge(probs_ready, UNITS * gi + 2 * s + 2 + CREDIT)
                pe.wait_ge(num_taken, SLOTS * gi + s - 1 + CREDIT)
                for cb in range(CB):
                    for h in range(2):
                        mm = nc.tensor.matmul(ps_n[s % 2][h * DH:(h + 1) * DH, :],
                                              v[:, CB * c + cb, (2 * p + h) * DH:(2 * p + h + 1) * DH],
                                              probs[:, (2 * s + h) % 4, cb * G:(cb + 1) * G],
                                              start=(cb == 0), stop=(cb == CB - 1))
                mm.then_inc(num_ready, 1)

            def denominator(gi, c):
                pe.wait_ge(presum_ready, UNITS * gi + HEADS * (c + 1) + CREDIT)
                if c % CHH == 0:
                    pe.wait_ge(den_taken, 2 * gi + c // CHH + CREDIT)
                for h in range(HEADS):
                    mm = nc.tensor.matmul(ps_d[32 * h:32 * (h + 1), :], pick[:, CHH - 1 - c % CHH:CHH + 31 - c % CHH],
                                          presum[:, c % 2 * HEADS + h, :], start=(c % CHH == 0), stop=(c % CHH == CHH - 1),
                                          tile_position=(0, 32 * h))
                mm.then_inc(den_sum, 1)

            def tail_out(gi, a):
                if a == 0:
                    pe.wait_ge(normed, SLOTS * (gi + 1) + CREDIT)
                pe.wait_ge(tail_taken, TURNS * gi + a + CREDIT)
                for t in range(2):
                    for k in range(KB):
                        at = (2 * a + t) * P
                        mm = nc.tensor.matmul(ps_x[:, t * F:(t + 1) * F], ctx_t[:, k, at:at + P], wo[:, k, :],
                                              start=(k == 0), stop=(k == KB - 1))
                mm.then_inc(tail_mm, 1)

            def tail_turn(gi, k):
                if k == 0:
                    pe.wait_ge(h1_ready, gi + 1 + CREDIT)
                pe.wait_ge(tail_taken, TURNS * gi + 2 + k + CREDIT)
                for t in range(T):
                    mm = nc.tensor.transpose(ps_x[:, t * P:(t + 1) * P], tg[:, t, k * P:(k + 1) * P], ident[:, :])
                mm.then_inc(tail_mm, 1)

            def project_1(dst, t, columns):
                n = 0
                for k in range(KB):
                    for a, c in PARTS:
                        mm = nc.tensor.matmul(dst, h1t[:, a, k, t * P:(t + 1) * P], w1s[:, c, k, columns],
                                              start=(n == 0), stop=(n == 3 * KB - 1))
                        n += 1
                return mm

            def tail_features(gi, a):
                pe.wait_ge(tail_taken, TURNS * gi + 4 + a + CREDIT)
                for t in range(2):
                    mm = project_1(ps_x[:, t * F:(t + 1) * F], 2 * a + t, slice(0, F))
                mm.then_inc(tail_mm, 1)

            def tail_s(gi):
                pe.wait_ge(tail_taken, TURNS * gi + 6 + CREDIT)
                for t in range(T):
                    mm = project_1(ps_x[:, 2 * t:2 * t + 2], t, slice(F, W1C))
                mm.then_inc(tail_mm, 1)

            def tail_early(gi, s):
                if s in (7, 8):
                    tail_out(gi, s - 7)
                if s == 15:
                    tail_features(gi, 1)

            def tail_step(gi, s):
                if s in (12, 13):
                    tail_turn(gi, s - 12)
                if s == 14:
                    tail_features(gi, 0)
                if s == 15:
                    tail_s(gi)

            def attend(gi, start, prev, more):
                if start:
                    score(gi, 0)
                    score(gi, 1)
                for s in range(SLOTS):
                    if s + 1 < SLOTS:
                        score(gi, 2 * s + 2)
                        score(gi, 2 * s + 3)
                    elif more:
                        score(gi + 1, 0)
                        score(gi + 1, 1)
                    if s == 0 and prev:
                        denominator(gi - 1, CH - 1)
                    if s > 0 and s % PAIRS == 0:
                        denominator(gi, s // PAIRS - 1)
                    if prev:
                        tail_early(gi - 1, s)
                    context(gi, s)
                    if prev:
                        tail_step(gi - 1, s)

            def aggregate(gi, g, mb):
                pe.wait_ge(prob1_ready, NB * gi + mb + 1 + CREDIT)
                for t in range(T):
                    if mb == 0:
                        pe.wait_ge(out_ready, T * (gi - 1) + t + 1 + CREDIT)
                    if mb == NB - 1:
                        for i in range(3):
                            nc.tensor.matmul(acc1[t], no_nb[:, bass.ds(g * G + t * P, P)], hs3[:, i, :],
                                             start=False, stop=False)
                    mm = nc.tensor.matmul(acc1[t], prob1[:, mb % 4, t * P:(t + 1) * P], h2[:, mb, :],
                                          start=(mb == 0), stop=(mb == NB - 1))
                    if mb == NB - 1:
                        mm.then_inc(agg_ready, 1)
                    elif t == T - 1:
                        mm.then_inc(prob1_used, 1)

            for task, n in PROJECT + LATE:
                task_a(0, task, n)
            pe.wait_ge(counted_blocks, NB + 1)
            pe.wait_ge(kq_ready, 4 * NG + CREDIT)
            for g in range(NG):
                mm = nc.tensor.matmul(ps_s[g // 2][:, G * (g % 2):G * (g % 2) + G], ones_bf[:, :],
                                      count[:, g * G:(g + 1) * G], start=True, stop=True)
            mm.then_inc(count_done, 1)
            pe.wait_ge(setup_done, 2)
            with pe.Fori(0, B) as b:
                pe.wait_ge(v_ready, 2 * (NG * b + NG) + CREDIT)
                pe.wait_ge(kq_ready, 4 * (NG * b + NG) + CREDIT)
                pe.wait_ge(out_ready, T * NG * b + CREDIT)
                pe.wait_ge(ks_in, 32 * (b + 1) + CREDIT)
                attend(NG * b, True, False, True)
                with pe.Fori(1, NG - 1) as g:
                    attend(NG * b + g, False, True, True)
                gl = NG * b + NG - 1
                attend(gl, False, True, False)
                denominator(gl, CH - 1)
                for task, n in BETWEEN:
                    task_a(gl + 1, task, n)
                    if task == "out":
                        tail_out(gl, n)
                    if task == "turn_h":
                        tail_turn(gl, n)
                    if task == "features":
                        tail_features(gl, n)
                    if task == "s":
                        tail_s(gl)
                pe.wait_ge(tail_taken, TURNS * (gl + 1) + CREDIT)
                nc.tensor.transpose(ps_x[0:NB, 0:P], s12[:, 0, :], ident[:, :]).then_inc(s1_turned, 1)
                for task, n in LATE:
                    task_a(gl + 1, task, n)
                pe.wait_ge(kq_ready, 4 * (gl + 1 + NG) + CREDIT)
                hold(pe)
                with pe.Fori(0, NG) as g:
                    for mb in range(NB):
                        if mb == NB - 1:
                            pe.wait_ge(hs_ready, b + 1 + CREDIT)
                            hold(pe)
                        aggregate(NG * b + g, g, mb)


def kernel(**inputs):
    import numpy as np
    import concourse.bacc as bacc
    from concourse.bass_utils import run_bass_kernel_spmd

    def t(a):
        return np.ascontiguousarray(np.asarray(a).T)

    p = {k.replace("L0_gnn_", "").replace("L1_gnn_", "L1_"): np.asarray(v) for k, v in inputs.items()}
    B, N, F = p["x"].shape
    host = {
        "x": p["x"], "adj_t": t(p["adj"]),
        "wq_t": t(p["Wq"]), "bq": p["bq"], "wk_t": t(p["Wk"]), "bk": p["bk"], "wv_t": t(p["Wv"]), "bv": p["bv"],
        "wo_t": t(p["Wo"]), "bo": p["bo"], "gamma": p["gamma"], "beta": p["beta"],
        "w1": p["L1_W"], "a1": p["L1_a"].reshape(2, F),
    }
    nc = bacc.Bacc("TRN2", target_bir_lowering=False, num_devices=1, dynamic_dma_scratch_size=1024)
    arrays, args = {}, []
    for name, a in host.items():
        a = np.ascontiguousarray(a)
        arrays[f"in_{name}"] = a
        args.append(nc.dram_tensor(f"in_{name}", a.shape, mybir.dt.from_np(a.dtype), kind="ExternalInput").ap())
    args.append(nc.dram_tensor("out_x", (B, N, F), F32, kind="ExternalOutput").ap())
    gnn_two_layers(nc, *args)
    r = run_bass_kernel_spmd(nc, [arrays], core_ids=[0])
    return r.results[0]["out_x"]
```
